# Optimizing a Trainium2 kernel written in Bass

```python
import numpy as np
import jax
import jax.numpy as jnp

def _softmax(x, axis=-1):
    return jax.nn.softmax(x, axis=axis)

def _gelu(x):
    return jax.nn.gelu(x, approximate=True)

def _silu(x):
    return jax.nn.silu(x)

def _sigmoid(x):
    return jax.nn.sigmoid(x)

def _layernorm(x, axis=-1, eps=1e-05):
    m = jnp.mean(x, axis=axis, keepdims=True)
    v = jnp.var(x, axis=axis, keepdims=True)
    return (x - m) / jnp.sqrt(v + eps)

def _scatter_add(tgt, idx, src, axis=0):
    return tgt.at[idx].add(src)

def _segment_sum(src, seg, n):
    return jax.ops.segment_sum(src, seg, n)
kernel_name = 'mk_gnn_ffn_d1_gnn_r8_e6b54f'

def setup_inputs(seed: int=0):
    np.random.seed(seed)
    _w = jnp.asarray

    def _rec_inputs():
        import jax
        import jax.numpy as jnp
        _gk = jax.random.key(seed)
        x = -0.0006008 + 1.001 * jax.random.normal(jax.random.fold_in(_gk, 1), (6250, 256), jnp.float32)
        src = jax.random.randint(jax.random.fold_in(_gk, 2), (100000,), 0, 6250, jnp.int32)
        dst = jax.random.randint(jax.random.fold_in(_gk, 3), (100000,), 0, 6250, jnp.int32)
        _o = jnp.argsort(dst, stable=True)
        src = src[_o]
        dst = dst[_o]
        return (x, src, dst)
    x, src, dst = _rec_inputs()

    def _L0_gnn_setup():
        import jax, jax.numpy as jnp
        import numpy as np
        N_NODES = 1250
        N_EDGES = 40000
        D_IN = 256
        D_OUT = 256
        key = jax.random.key(seed)
        k1, k2, k3, k4 = jax.random.split(key, 4)
        x = jax.random.normal(k1, (N_NODES, D_IN), dtype=jnp.float32)
        edge_index = jax.random.randint(k2, (2, N_EDGES), 0, N_NODES, dtype=jnp.int64)
        weight = jax.random.normal(k3, (2 * D_IN, D_OUT), dtype=jnp.float32) / np.sqrt(2 * D_IN)
        bias = jax.random.normal(k4, (D_OUT,), dtype=jnp.float32)
        return {'x': x, 'edge_index': edge_index, 'weight': weight, 'bias': bias}
    _L0_gnn_all = _L0_gnn_setup()
    _L0_gnn_in = {k: v for k, v in _L0_gnn_all.items() if k in ('weight', 'bias')}
    del _L0_gnn_all

    def _L0_ffn_setup():
        import math
        import jax, jax.numpy as jnp
        import numpy as np
        CAPACITY_FACTOR = 1.25
        key = jax.random.key(seed)
        ks = jax.random.split(key, 5)
        B, L, D, F, E = (8, 1024, 256, 1024, 8)
        h = jax.random.normal(ks[0], (B, L, D), dtype=jnp.float32)
        gate_w = jax.random.normal(ks[1], (D, E), dtype=jnp.float32) * 0.02
        gate_b = jnp.zeros((E,), dtype=jnp.float32)
        w1 = jax.random.normal(ks[2], (E, D, F), dtype=jnp.float32) * (1.0 / math.sqrt(D))
        b1 = jnp.zeros((E, F), dtype=jnp.float32)
        w2 = jax.random.normal(ks[3], (E, F, D), dtype=jnp.float32) * (1.0 / math.sqrt(F))
        b2 = jnp.zeros((E, D), dtype=jnp.float32)
        return {'h': h, 'gate_w': gate_w, 'gate_b': gate_b, 'w1': w1, 'b1': b1, 'w2': w2, 'b2': b2}
    _L0_ffn_all = _L0_ffn_setup()
    _L0_ffn_in = {k: v for k, v in _L0_ffn_all.items() if k in ('gate_w', 'gate_b', 'w1', 'b1', 'w2', 'b2')}
    del _L0_ffn_all
    return {'x': x, 'src': src, 'dst': dst, 'L0_gnn_weight': _L0_gnn_in['weight'], 'L0_gnn_bias': _L0_gnn_in['bias'], 'L0_ffn_gate_w': _L0_ffn_in['gate_w'], 'L0_ffn_gate_b': _L0_ffn_in['gate_b'], 'L0_ffn_w1': _L0_ffn_in['w1'], 'L0_ffn_b1': _L0_ffn_in['b1'], 'L0_ffn_w2': _L0_ffn_in['w2'], 'L0_ffn_b2': _L0_ffn_in['b2']}

def reference(x, src, dst, L0_gnn_weight, L0_gnn_bias, L0_ffn_gate_w, L0_ffn_gate_b, L0_ffn_w1, L0_ffn_b1, L0_ffn_w2, L0_ffn_b2):
    import jax
    import jax.numpy as jnp

    def _L0_gnn_ref(x, edge_index, weight, bias):
        import jax, jax.numpy as jnp
        import numpy as np
        N_NODES = 1250
        N_EDGES = 40000
        D_IN = 256
        D_OUT = 256
        n = x.shape[0]
        src, dst = (edge_index[0], edge_index[1])
        summed = jax.ops.segment_sum(x[src], dst, num_segments=n)
        deg = jax.ops.segment_sum(jnp.ones_like(src, dtype=x.dtype), dst, num_segments=n)
        agg = summed / jnp.maximum(deg, 1.0)[:, None]
        out = jnp.concatenate([x, agg], axis=-1) @ weight
        out = out / jnp.linalg.norm(out, axis=-1, keepdims=True)
        return out + bias

    def _L0_ffn_ref(h, gate_w, gate_b, w1, b1, w2, b2):
        import math
        import jax, jax.numpy as jnp
        import numpy as np
        CAPACITY_FACTOR = 1.25
        B, L, D = h.shape
        E = gate_w.shape[1]
        T = B * L
        C = max(1, math.ceil(CAPACITY_FACTOR * T / E))
        x = h.reshape(T, D)
        logits = x @ gate_w + gate_b
        probs = jax.nn.softmax(logits, axis=-1)
        idx = jnp.argmax(probs, axis=-1)
        prb = jnp.take_along_axis(probs, idx[:, None], axis=1)[:, 0]
        one_hot = jax.nn.one_hot(idx, E, dtype=jnp.float32)
        pos = (jnp.cumsum(one_hot, axis=0) * one_hot).sum(-1).astype(jnp.int32) - 1
        kept = pos < C
        pos_safe = jnp.where(kept, pos, C)
        buf = jnp.zeros((E, C, D), dtype=h.dtype).at[idx, pos_safe].set(x, mode='drop')
        hmid = jax.nn.relu(jnp.einsum('ecd,edf->ecf', buf, w1) + b1[:, None, :])
        ybuf = jnp.einsum('ecf,efd->ecd', hmid, w2) + b2[:, None, :]
        pos_g = jnp.minimum(pos, C - 1)
        y_tok = ybuf[idx, pos_g] * (prb * kept)[:, None]
        y = y_tok.reshape(B, L, D)
        y = jnp.nan_to_num(y, nan=0.0, posinf=10000.0, neginf=-10000.0)
        return y
    edge_index = jnp.stack([src, dst])
    x = x + _L0_gnn_ref(_layernorm(x, axis=-1), edge_index, L0_gnn_weight, L0_gnn_bias)
    x = x + _L0_ffn_ref(_layernorm(x, axis=-1)[None], L0_ffn_gate_w, L0_ffn_gate_b, L0_ffn_w1, L0_ffn_b1, L0_ffn_w2, L0_ffn_b2)[0]
    return x

_drawn_inputs = setup_inputs


def setup_inputs(seed=0):
    import zlib

    import numpy as np

    out = dict(_drawn_inputs(seed))
    spreads = {'L0_ffn_gate_b': (0.0, 0.1), 'L0_ffn_b1': (0.0, 0.8), 'L0_ffn_b2': (0.0, 0.8)}
    factors = {}
    for name, (base, spread) in spreads.items():
        noise = np.random.default_rng([zlib.crc32(name.encode()), seed]).standard_normal(out[name].shape)
        drawn = base * np.exp(spread * noise) if base else spread * noise
        out[name] = jnp.asarray(drawn.astype(out[name].dtype))
    for name, factor in factors.items():
        out[name] = (out[name] * factor).astype(out[name].dtype)
    return out
```

```python
import numpy as np
import concourse.bass as bass
from concourse import mybir
from contextlib import ExitStack

FP32 = mybir.dt.float32
BF16 = mybir.dt.bfloat16
I32 = mybir.dt.int32
I16 = mybir.dt.int16
ALU = mybir.AluOpType
ACT = mybir.ActivationFunctionType
AX = mybir.AxisListType.X

P = 128
N = 6250
D = 256
E_EDGES = 100000
NB = -(-N // P)
LAST = N - (NB - 1) * P
TQ = 4
QE = TQ * P
QH = 98
NQ = 2 * QH
QS = 4
FULLQ = E_EDGES // QE
TAIL = E_EDGES - FULLQ * QE
PAD_DST = 16383
NPART = 3
XG = 7
NG = NB // XG
EX = 8
F = 1024
JF = F // P
KD = D // P
CAP = -(-5 * N // (4 * EX))
CH = -(-CAP // P)
SLOTS = CH * P
ROW = 260
C_MEAN, C_RSTD, C_GATE, C_NODE = D, D + 1, D + 2, D + 3
EPS = 1e-5
AW = D + 1


def gnn_moe_layer(nc, x, src, dst, gnn_w, gnn_b, gate_w, gate_b, w1, b1, w2, b2, out):
    ds = bass.ds
    parts_d = nc.dram_tensor("parts_d", (N, NPART * D), BF16, kind="Internal").ap()
    disp_d = nc.dram_tensor("disp_d", (EX * SLOTS, ROW), FP32, kind="Internal").ap()

    ctx = ExitStack()
    with ctx:
        def sb(name, shape, dt):
            return ctx.enter_context(nc.sbuf_tensor(name, shape, dt))

        def pb(name, shape):
            return ctx.enter_context(nc.psum_tensor(name, shape, FP32))

        def sem(name):
            return ctx.enter_context(nc.semaphore(name))

        w1_sb = sb("w1_sb", [P, KD, EX * F], FP32)
        w2_sb = sb("w2_sb", [P, JF, EX * D], FP32)
        acc = sb("acc", [P, NB * AW], FP32)
        ring = sb("ring", [P, 2 * TQ, NPART * D], BF16)
        dst_t = sb("dst_t", [P, NQ, TQ], I16)
        src_t = sb("src_t", [P, NQ + 3, TQ], I16)
        idx = sb("idx", [P, QS * TQ], I32)
        rel = sb("rel", [P, 2, TQ], FP32)
        sel = sb("sel", [P, 2, TQ, P], BF16)
        ident = sb("ident", [P, P], FP32)
        tri = sb("tri", [P, P], BF16)
        ones = sb("ones", [P, P], BF16)
        ones_bf = sb("ones_bf", [P, 1], BF16)
        lane = sb("lane", [P, P], BF16)
        block0 = sb("block0", [P, NB], FP32)
        node_id = sb("node_id", [P, NB], FP32)
        rev = sb("rev", [P, EX], FP32)
        mean1 = sb("mean1", [P, NB], FP32)
        rstd1 = sb("rstd1", [P, NB], FP32)
        gw_sb = sb("gw_sb", [P, 2 * KD, D], FP32)
        gb_sb = sb("gb_sb", [P, D], FP32)
        gatew_sb = sb("gatew_sb", [P, KD, EX], FP32)
        gateb_sb = sb("gateb_sb", [P, EX], FP32)
        b1_t = sb("b1_t", [P, EX * JF], FP32)
        qtab = sb("qtab", [1, NQ, 2], I16)
        seen = sb("seen", [P, EX], FP32)
        xb = sb("xb", [P, D], FP32)
        cat = sb("cat", [P, 2 * D], FP32)
        cat_t = sb("cat_t", [P, 2 * KD, P], FP32)
        row = sb("row", [P, ROW], FP32)
        slot = sb("slot", [P, 1], I32)
        sm = sb("sm", [P, 32], FP32)
        g8 = sb("g8", [P, 8, EX], FP32)
        hot = sb("hot", [P, EX], BF16)
        bn = sb("bn", [P, 6], FP32)
        crow = sb("crow", [P, ROW], FP32)
        b2_b = sb("b2_b", [P, D], FP32)
        hid = sb("hid", [P, F], FP32)
        hid_t = sb("hid_t", [P, JF, P], FP32)
        xc_t = hid_t[:, 0:KD, :]
        res = hid[:, D:2 * D]
        node_i = sb("node_i", [P, 1], I32)

        w1_flat = w1_sb[:, :, :].rearrange("p k f -> p (k f)")
        w2_flat = w2_sb[:, :, :].rearrange("p j f -> p (j f)")

        def carve(flat, at, n):
            return flat[:, at:at + n]

        XW = XG * D
        xin = [carve(w1_flat, s * XW, XW) for s in range(2)]
        xn = [carve(w1_flat, (2 + s) * XW, XW) for s in range(2)]
        r1 = [carve(w1_flat, (4 + s) * XW, XW) for s in range(2)]
        parts = [carve(w2_flat, s * NPART * XW // 2, NPART * XW // 2).bitcast(BF16) for s in range(2)]
        at = NPART * XW
        dst_i = carve(w2_flat, at, 2 * QE).bitcast(I32)
        src_i = carve(w2_flat, at + 2 * QE, 2 * QE).bitcast(I32)
        dst_f = carve(w2_flat, at + 4 * QE, 2 * QE)
        src_f = carve(w2_flat, at + 6 * QE, 2 * QE)
        dst_m = carve(w2_flat, at + 8 * QE, 2 * QE)
        b1_r = w1_flat[0:EX * JF, 6 * XW:6 * XW + P]
        qmm = carve(w2_flat, at + 10 * QE, 4)
        qmi = carve(w2_flat, at + 10 * QE + 8, 4).bitcast(I32)
        qmf = carve(w2_flat, at + 10 * QE + 16, 4)
        bn1 = carve(w1_flat, 6 * XW + P, XG * 6)
        mv1 = carve(w1_flat, 6 * XW + P + 64, XG * 2)
        nt1 = carve(w1_flat, 6 * XW + P + 96, XG * 2)

        ps_q = [pb(f"ps_q{i}", [P, 512]) for i in range(2)]
        ps_a = pb("ps_a", [P, 4, P])
        ps_b = pb("ps_b", [P, 512])
        ps_h = pb("ps_h", [P, F])
        ps_t = pb("ps_t", [P, JF, P])

        stage_clear = sem("stage_clear")
        stage_in = sem("stage_in")
        const_in = sem("const_in")
        b1_in = sem("b1_in")
        consts = sem("consts")
        pool_step = sem("pool_step")
        pool_turn = sem("pool_turn")
        xin_in = [sem(f"xin_in{s}") for s in range(2)]
        xin_used = sem("xin_used")
        var1_ready = sem("var1_ready")
        ln1_ready = sem("ln1_ready")
        xn_ready = sem("xn_ready")
        r1_ready = sem("r1_ready")
        hi_copied = sem("hi_copied")
        low_done = sem("low_done")
        parts_out = [sem(f"parts_out{s}") for s in range(2)]
        stage_f = sem("stage_f")
        edges_t = sem("edges_t")
        edges_copied = sem("edges_copied")
        qblocks = sem("qblocks")
        qrow = sem("qrow")
        qtab_ready = sem("qtab_ready")
        acc_clear = sem("acc_clear")
        weights_in = sem("weights_in")
        disp_clear = sem("disp_clear")
        idx_ready = sem("idx_ready")
        gathered = [sem(f"gathered{s}") for s in range(2)]
        ring_free = sem("ring_free")
        sel_ready = sem("sel_ready")
        visit_done = sem("visit_done")
        acc_done = sem("acc_done")
        edges_done = sem("edges_done")
        xb_in = sem("xb_in")
        xb_free = sem("xb_free")
        cat_ready = sem("cat_ready")
        cat_ps = sem("cat_ps")
        catt_ready = sem("catt_ready")
        z_ready = sem("z_ready")
        zln_ready = sem("zln_ready")
        x1_ready = sem("x1_ready")
        var2_ready = sem("var2_ready")
        ln2_ready = sem("ln2_ready")
        xl_ready = sem("xl_ready")
        xl_ps = sem("xl_ps")
        xlt_ready = sem("xlt_ready")
        logit_ps = sem("logit_ps")
        logit_ready = sem("logit_ready")
        exp_ready = sem("exp_ready")
        hot_ready = sem("hot_ready")
        count_ps = sem("count_ps")
        row_ready = sem("row_ready")
        x1_out = sem("x1_out")
        disp_out = sem("disp_out")
        row_free = sem("row_free")
        crow_in = sem("crow_in")
        crow_free = sem("crow_free")
        xc_ready = sem("xc_ready")
        xc_ps = sem("xc_ps")
        xct_ready = sem("xct_ready")
        hid_ps = sem("hid_ps")
        hid_ready = sem("hid_ready")
        hidt_ps = sem("hidt_ps")
        hidt_ready = sem("hidt_ready")
        y_ready = sem("y_ready")
        res_ready = sem("res_ready")
        res_out = sem("res_out")

        block = ctx.enter_context(nc.Block())

        def rows_of(b, n=P):
            return ds(b * P, n)

        @block.sync
        def _(sp):
            sp.wait_ge(stage_clear, 1)
            for dram, staged in ((dst, dst_i), (src, src_i)):
                sp.dma_start(staged[0:QH, 0:QE],
                             dram[0:QH * QE].rearrange("(p e) -> p e", e=QE)).then_inc(stage_in, 16)
                sp.dma_start(staged[0:FULLQ - QH, QE:2 * QE],
                             dram[QH * QE:FULLQ * QE].rearrange("(p e) -> p e", e=QE)).then_inc(stage_in, 16)
                sp.dma_start(staged[FULLQ - QH:FULLQ - QH + 1, QE:QE + TAIL],
                             dram[FULLQ * QE:E_EDGES].rearrange("(p e) -> p e", p=1)).then_inc(stage_in, 16)
            sp.dma_start(b1_r, b1.rearrange("e (j p) -> (e j) p", p=P)).then_inc(b1_in, 16)

            def load_x(g, s, blocks):
                sp.dma_start(xin[s][:, 0:blocks * D].rearrange("p (b d) -> p b d", d=D),
                             x[ds(g * (XG * P), blocks * P), :].rearrange("(b p) d -> p b d", p=P)
                             ).then_inc(xin_in[s], 16)

            def store_parts(g, s, blocks):
                sp.dma_start(parts_d[ds(g * (XG * P), blocks * P), :].rearrange("(b p) d -> p b d", p=P),
                             parts[s][:, 0:blocks * NPART * D].rearrange("p (b d) -> p b d", d=NPART * D)
                             ).then_inc(parts_out[s], 16)

            load_x(0, 0, XG)
            load_x(1, 1, XG)
            for g in range(NG):
                s = g % 2
                sp.wait_ge(low_done, g + 1)
                sp.wait_ge(hi_copied, g + 1)
                if g < NG - 1:
                    store_parts(g, s, XG)
                else:
                    store_parts(g, s, XG - 1)
                    sp.dma_start(parts_d[(NB - 1) * P:N, :],
                                 parts[s][0:LAST, (XG - 1) * NPART * D:XG * NPART * D]).then_inc(parts_out[s], 16)
                if g + 2 < NG:
                    sp.wait_ge(xin_used, g + 1)
                    load_x(g + 2, s, XG if g + 2 < NG - 1 else XG - 1)
                    if g + 2 == NG - 1:
                        sp.dma_start(xin[s][0:LAST, (XG - 1) * D:XG * D], x[(NB - 1) * P:N, :]
                                     ).then_inc(xin_in[s], 16)
            sp.wait_ge(parts_out[0], 16 * (NG // 2 + 2))
            sp.wait_ge(parts_out[1], 16 * (NG // 2))
            sp.wait_ge(qtab_ready, 1)
            sp.wait_ge(edges_copied, 5)
            for k in range(KD):
                sp.dma_start(w1_sb[:, k, :].rearrange("p (e f) -> p e f", f=F),
                             w1[:, k * P:(k + 1) * P, :].rearrange("e p f -> p e f")).then_inc(weights_in, 16)
            for j in range(JF):
                sp.dma_start(w2_sb[:, j, :].rearrange("p (e f) -> p e f", f=D),
                             w2[:, j * P:(j + 1) * P, :].rearrange("e p f -> p e f")).then_inc(weights_in, 16)

            sp.wait_ge(consts, 1)
            sp.dma_start(disp_d.rearrange("(t p) c -> p t c", p=P),
                         row[:, :].rearrange("p (a c) -> p a c", a=1).to_broadcast((P, EX * CH, ROW))
                         ).then_inc(disp_clear, 16)

            def load_node(i, rows):
                sp.wait_ge(xb_free, i + 1)
                sp.dma_start(xb[0:rows, :], x[rows_of(i, rows), :]).then_inc(xb_in, 16)

            def node_out(i, rows):
                sp.wait_ge(x1_ready, i + 1)
                sp.dma_start(out[rows_of(i, rows), :], row[0:rows, 0:D]).then_inc(x1_out, 16)
                sp.wait_ge(x1_out, 16 * (i + 1))
                sp.wait_ge(disp_out, 16 * (i + 1))
                sp.sem_inc(row_free, 1)

            sp.wait_ge(disp_clear, 16)
            sp.sem_inc(row_free, 1)
            with sp.Fori(0, NB - 1) as i:
                load_node(i, P)
                node_out(i, P)
            load_node(NB - 1, LAST)
            node_out(NB - 1, LAST)

            with sp.Fori(0, EX) as e:
                with sp.Fori(0, CH) as c:
                    i = e * CH + c
                    sp.wait_ge(crow_free, i + 1)
                    sp.dma_start(crow[:, :], disp_d[ds(e * SLOTS + c * P, P), :]).then_inc(crow_in, 16)
                    sp.dma_start(b2_b[:, :], b2[ds(e, 1), :].to_broadcast((P, D))).then_inc(crow_in, 16)
                    sp.wait_ge(res_out, 16 * (i + 1))
                    sp.sem_inc(crow_free, 1)

        @block.gpsimd
        def _(pool):
            pool.memset(dst_i[:, :], PAD_DST)
            pool.memset(src_i[:, :], 0).then_inc(stage_clear, 1)
            pool.memset(ident[:, :], 0.0)
            pool.memset(tri[:, :], 1.0)
            pool.memset(ones[:, :], 1.0)
            pool.memset(seen[:, :], 0.0)
            pool.memset(row[:, 0:C_NODE], 0.0)
            pool.memset(row[:, C_NODE:C_NODE + 1], float(1 << 20))
            pool.memset(xb[:, :], 0.0)
            pool.memset(ones_bf[:, :], 1.0).then_inc(pool_step, 1)
            pool.iota(lane[:, :], [[1, P]], base=0, channel_multiplier=0, allow_small_or_imprecise_dtypes=True)
            pool.iota(block0[:, :], [[P, NB]], base=0, channel_multiplier=0, allow_small_or_imprecise_dtypes=True)
            pool.iota(node_id[:, :], [[P, NB]], base=0, channel_multiplier=1, allow_small_or_imprecise_dtypes=True)
            pool.iota(rev[:, :], [[-1, EX]], base=EX, channel_multiplier=0, allow_small_or_imprecise_dtypes=True)
            pool.wait_ge(pool_step, 1)
            pool.affine_select(out=ident[:, :], in_=ident[:, :], compare_op=ALU.not_equal, fill=1.0,
                               base=0, pattern=[[-1, P]], channel_multiplier=1)
            pool.affine_select(out=tri[:, :], in_=tri[:, :], compare_op=ALU.is_ge, fill=0.0,
                               base=0, pattern=[[1, P]], channel_multiplier=-1).then_inc(consts, 1)
            for view, dram in ((gb_sb[:, :], gnn_b.rearrange("(a n) -> a n", a=1).to_broadcast((P, D))),
                               (gateb_sb[:, :], gate_b.rearrange("(a n) -> a n", a=1).to_broadcast((P, EX))),
                               (gw_sb[:, :, :], gnn_w.rearrange("(k p) n -> p k n", p=P)),
                               (gatew_sb[:, :, :], gate_w.rearrange("(k p) n -> p k n", p=P))):
                pool.dma_start(view, dram).then_inc(const_in, 16)
            for g in range(NG):
                s = g % 2
                pool.wait_ge(r1_ready, g + 1)
                if g >= 2:
                    pool.wait_ge(parts_out[s], 16 * (g // 2))
                pool.tensor_tensor(
                    out=parts[s][:, :].rearrange("p (b k d) -> p b k d", k=NPART, d=D)[:, :, 2, :],
                    in0=r1[s][:, :].rearrange("p (b d) -> p b d", d=D),
                    in1=r1[s][:, :].bitcast(BF16).rearrange("p (b d t) -> p b d t", d=D, t=2)[:, :, :, 1],
                    op=ALU.subtract).then_inc(low_done, 1)
            pool.wait_ge(parts_out[0], 16 * (NG // 2 + 2))
            pool.wait_ge(parts_out[1], 16 * (NG // 2))
            with pool.Fori(0, NQ // QS) as u:
                for k in range(QS):
                    turn = pool.snap(u * QS + (k + 1))
                    pool.wait_ge(idx_ready, turn)
                    pool.wait_ge(ring_free, turn)
                    pool.sem_inc(pool_turn, 1)
                    for j in range(TQ):
                        pool.indirect_dma_start(
                            ring[:, (k % 2) * TQ + j, :], None, parts_d[:, :],
                            bass.IndirectOffsetOnAxis(ap=idx[:, k * TQ + j:k * TQ + j + 1], axis=0)
                        ).then_inc(gathered[k % 2], 16)

            def dispatch(i, rows):
                pool.wait_ge(row_ready, i + 1)
                pool.sem_inc(pool_turn, 1)
                pool.indirect_dma_start(
                    disp_d[:, :], bass.IndirectOffsetOnAxis(ap=slot[0:rows, 0:1], axis=0), row[0:rows, :], None,
                    bounds_check=EX * SLOTS - 1, oob_is_err=False).then_inc(disp_out, 16)

            with pool.Fori(0, NB - 1) as i:
                dispatch(i, P)
            dispatch(NB - 1, LAST)
            pool.wait_ge(x1_out, 16 * NB)
            with pool.Fori(0, EX * CH) as i:
                pool.wait_ge(res_ready, i + 1)
                pool.sem_inc(pool_turn, 1)
                pool.indirect_dma_start(
                    out[:, :], bass.IndirectOffsetOnAxis(ap=node_i[:, 0:1], axis=0), res, None,
                    bounds_check=N - 1, oob_is_err=False).then_inc(res_out, 16)
            pool.wait_ge(res_out, 16 * EX * CH)

        @block.scalar
        def _(act):
            def rsqrt_start(to, of, tmp):
                act.activation(tmp, of, ACT.Ln)
                act.drain()
                return act.activation(to, tmp, ACT.Exp, scale=-0.5)

            act.preload_act_table_set("natural_log_exp_and_others")
            act.wait_ge(consts, 1)
            for g in range(NG):
                s = g % 2
                act.wait_ge(var1_ready, g + 1)
                rsqrt_start(nt1[:, XG:2 * XG], mv1[:, 1:2 * XG:2], nt1[:, 0:XG]).then_inc(ln1_ready, 1)
                view = parts[s][:, :].rearrange("p (b k d) -> p b k d", k=NPART, d=D)
                act.wait_ge(xn_ready, g + 1)
                if g >= 2:
                    act.wait_ge(parts_out[s], 16 * (g // 2))
                act.activation(view[:, :, 0, :],
                               xn[s][:, :].bitcast(BF16).rearrange("p (b d t) -> p b d t", d=D, t=2)[:, :, :, 1],
                               ACT.Copy)
                act.wait_ge(r1_ready, g + 1)
                act.activation(view[:, :, 1, :],
                               r1[s][:, :].bitcast(BF16).rearrange("p (b d t) -> p b d t", d=D, t=2)[:, :, :, 1],
                               ACT.Copy).then_inc(hi_copied, 1)

            def node(i):
                act.wait_ge(cat_ps, i + 1)
                act.activation(cat_t[:, :, :], ps_a[:, :, :], ACT.Copy).then_inc(catt_ready, 1)
                act.wait_ge(z_ready, i + 1)
                act.activation(cat[:, 0:D], ps_b[:, 0:D], ACT.Square, accum_out=sm[:, 0:1])
                act.drain()
                rsqrt_start(sm[:, 2:3], sm[:, 0:1], sm[:, 1:2]).then_inc(zln_ready, 1)
                act.wait_ge(var2_ready, i + 1)
                rsqrt_start(sm[:, 12:13], sm[:, 10:11], sm[:, 11:12]).then_inc(ln2_ready, 1)
                act.wait_ge(xl_ps, i + 1)
                act.activation(cat_t[:, 0:KD, :], ps_a[:, 0:KD, :], ACT.Copy).then_inc(xlt_ready, 1)
                act.wait_ge(logit_ready, i + 1)
                act.activation(g8[:, 1, :], g8[:, 0, :], ACT.Exp, bias=sm[:, 16:17],
                               accum_out=sm[:, 17:18]).then_inc(exp_ready, 1)

            with act.Fori(0, NB - 1) as i:
                node(i)
            node(NB - 1)
            with act.Fori(0, EX) as e:
                with act.Fori(0, CH) as c:
                    i = e * CH + c
                    act.wait_ge(xc_ps, i + 1)
                    act.activation(xc_t, ps_a[:, 0:KD, :], ACT.Copy).then_inc(xct_ready, 1)
                    act.wait_ge(hid_ps, 2 * i + 2)
                    act.activation(hid[:, 512:F], ps_h[:, 512:F], ACT.Copy).then_inc(hid_ready, 1)
                    for h in range(2):
                        act.wait_ge(hidt_ps, 2 * i + h + 1)
                        for j in range(h * 4, h * 4 + 4):
                            last = act.activation(hid_t[:, j, :], ps_t[:, j, :], ACT.Relu,
                                                  bias=b1_t[:, ds(e * JF + j, 1)])
                        last.then_inc(hidt_ready, 1)

        @block.tensor
        def _(pe):
            pe.sem_inc(ring_free, 2)
            pe.sem_inc(visit_done, 2)
            pe.wait_ge(consts, 1)
            pe.wait_ge(stage_f, 1)
            for m, staged in enumerate((dst_f, src_f)):
                for h in range(2):
                    if m or h:
                        pe.wait_ge(edges_copied, 2 * m + h)
                    for j in range(TQ):
                        last = pe.transpose(ps_a[:, j, 0:QH], staged[0:QH, h * QE + j * P:h * QE + (j + 1) * P],
                                            ident[0:QH, 0:QH])
                    last.then_inc(edges_t, 1)
            pe.wait_ge(b1_in, 16)
            pe.wait_ge(edges_copied, 4)
            pe.transpose(ps_a[:, 0, 0:EX * JF], b1_r, ident[0:EX * JF, 0:EX * JF]).then_inc(edges_t, 1)
            pe.wait_ge(qblocks, 1)
            for m in range(4):
                last = pe.matmul(ps_b[0:1, m * QH:(m + 1) * QH], qmf[0:QH, m:m + 1], ident[0:QH, 0:QH],
                                 start=True, stop=True)
            last.then_inc(qrow, 1)

            n = pe.alloc_register("visits")
            b = pe.alloc_register("visit_block")
            pe.reg_mov(n, 0)
            regs = [pe.alloc_register(f"quad_blocks{i}") for i in range(2 * QS)]
            pe.wait_ge(qtab_ready, 1)

            def visit(k, s, final):
                ps = ps_q[s]
                for j in range(TQ):
                    for part in range(NPART):
                        mm = pe.matmul(ps[:, 0:D], sel[:, s, j, :],
                                       ring[:, (k % 2) * TQ + j, part * D:(part + 1) * D],
                                       start=(j == 0 and part == 0), stop=(j == TQ - 1 and part == NPART - 1),
                                       skip_group_check=True)
                    if final and j == TQ - 1:
                        mm.then_inc(ring_free, 1)
                    mm = pe.matmul(ps[:, D:AW], sel[:, s, j, :], ones_bf[:, :], start=False,
                                   stop=(j == TQ - 1), skip_group_check=True)
                mm.then_inc(visit_done, 1)

            with pe.Fori(0, NQ // QS) as u:
                pe.load(regs, qtab[0:1, ds(u * QS, QS), :])
                for k in range(QS):
                    pe.reg_mov(b, regs[2 * k])
                    pe.wait_ge(gathered[k % 2], 16 * TQ * ((QS // 2) * u + k // 2 + 1))
                    with pe.While(lambda: pe.snap(b) < pe.snap(regs[2 * k + 1])):
                        pe.wait_ge(sel_ready, pe.snap(n) + 1)
                        pe.wait_ge(acc_done, pe.snap(n) + 2)
                        visit(k, (k + 1) % 2, False)
                        pe.reg_add(n, n, 1)
                        pe.reg_add(b, b, 1)
                    pe.wait_ge(sel_ready, pe.snap(n) + 1)
                    pe.wait_ge(acc_done, pe.snap(n) + 1)
                    visit(k, k % 2, True)
                    pe.reg_add(n, n, 1)

            def node(i, rows):
                pe.wait_ge(cat_ready, i + 1)
                for k in range(2 * KD):
                    last = pe.transpose(ps_a[:, k, :], cat[:, k * P:(k + 1) * P], ident[:, :])
                last.then_inc(cat_ps, 1)
                pe.wait_ge(catt_ready, i + 1)
                for k in range(2 * KD):
                    last = pe.matmul(ps_b[:, 0:D], cat_t[:, k, :], gw_sb[:, k, :],
                                     start=(k == 0), stop=(k == 2 * KD - 1))
                last.then_inc(z_ready, 1)
                pe.wait_ge(xl_ready, i + 1)
                for k in range(KD):
                    last = pe.transpose(ps_a[:, k, :], cat[:, D + k * P:D + (k + 1) * P], ident[:, :])
                last.then_inc(xl_ps, 1)
                pe.wait_ge(xlt_ready, i + 1)
                for k in range(KD):
                    last = pe.matmul(ps_b[:, D:D + EX], cat_t[:, k, :], gatew_sb[:, k, :],
                                     start=(k == 0), stop=(k == KD - 1))
                last.then_inc(logit_ps, 1)
                pe.wait_ge(hot_ready, i + 1)
                pe.matmul(ps_b[:, D + EX:D + 2 * EX], tri[0:rows, :], hot[0:rows, :], start=True, stop=True)
                pe.matmul(ps_b[:, D + 2 * EX:D + 3 * EX], ones[0:rows, :], hot[0:rows, :],
                          start=True, stop=True).then_inc(count_ps, 1)

            with pe.Fori(0, NB - 1) as i:
                node(i, P)
            node(NB - 1, LAST)

            pe.wait_ge(weights_in, 16 * (KD + JF))
            with pe.Fori(0, EX) as e:
                with pe.Fori(0, CH) as c:
                    i = e * CH + c
                    pe.wait_ge(xc_ready, i + 1)
                    for k in range(KD):
                        last = pe.transpose(ps_a[:, k, :], hid[:, k * P:(k + 1) * P], ident[:, :])
                    last.then_inc(xc_ps, 1)
                    pe.wait_ge(xct_ready, i + 1)
                    for h in range(2):
                        for k in range(KD):
                            last = pe.matmul(ps_h[:, h * 512:(h + 1) * 512], xc_t[:, k, :],
                                             w1_sb[:, k, ds(e * F + h * 512, 512)],
                                             start=(k == 0), stop=(k == KD - 1))
                        last.then_inc(hid_ps, 1)
                    pe.wait_ge(hid_ready, 2 * i + 2)
                    for h in range(2):
                        for j in range(h * 4, h * 4 + 4):
                            last = pe.transpose(ps_t[:, j, :], hid[:, j * P:(j + 1) * P], ident[:, :])
                        last.then_inc(hidt_ps, 1)
                    for j in range(JF):
                        if j % 4 == 0:
                            pe.wait_ge(hidt_ready, 2 * i + j // 4 + 1)
                        last = pe.matmul(ps_b[:, 0:D], hid_t[:, j, :], w2_sb[:, j, ds(e * D, D)],
                                         start=(j == 0), stop=(j == JF - 1))
                    last.then_inc(y_ready, 1)

        @block.vector
        def _(dve):
            def newton(to, v, r, tmp):
                dve.tensor_tensor(tmp, v, r, ALU.mult)
                dve.drain()
                dve.tensor_tensor(tmp, tmp, r, ALU.mult)
                dve.drain()
                dve.tensor_scalar(tmp, tmp, -0.5, 1.5, ALU.mult, ALU.add)
                dve.drain()
                return dve.tensor_tensor(to, tmp, r, ALU.mult)

            dve.sem_inc(acc_done, 1)
            dve.memset(acc[:, :], 0.0)
            dve.memset(src_t[:, NQ:NQ + 3, :], 0)
            dve.memset(ps_q[1][:, 0:AW], 0.0)
            dve.wait_ge(stage_in, 16 * 6)
            dve.tensor_copy(dst_f[0:QH, :], dst_i[0:QH, :])
            dve.tensor_copy(src_f[0:QH, :], src_i[0:QH, :]).then_inc(stage_f, 1)
            dve.drain()
            dve.scalar_tensor_tensor(out=dst_m[0:QH, :], in0=dst_f[0:QH, :], scalar=float(N), in1=dst_f[0:QH, :],
                                     op0=ALU.is_lt, op1=ALU.mult)
            dve.drain()
            dve.tensor_reduce(qmm[0:QH, 0:2], dst_f[0:QH, :].rearrange("p (h e) -> p h e", h=2), AX, ALU.min)
            dve.tensor_reduce(qmm[0:QH, 2:4], dst_m[0:QH, :].rearrange("p (h e) -> p h e", h=2), AX, ALU.max)
            dve.drain()
            dve.tensor_copy(qmi[0:QH, :], qmm[0:QH, :])
            dve.drain()
            dve.tensor_scalar(qmi[0:QH, :], qmi[0:QH, :], 7, None, ALU.logical_shift_right)
            dve.drain()
            dve.tensor_copy(qmf[0:QH, :], qmi[0:QH, :]).then_inc(qblocks, 1)
            for m, to in enumerate((dst_t, src_t)):
                for h in range(2):
                    dve.wait_ge(edges_t, 2 * m + h + 1)
                    dve.tensor_copy(to[:, h * QH:(h + 1) * QH, :].rearrange("p q j -> p j q"),
                                    ps_a[:, :, 0:QH]).then_inc(edges_copied, 1)
            dve.wait_ge(edges_t, 5)
            dve.tensor_copy(b1_t[:, :], ps_a[:, 0, 0:EX * JF]).then_inc(edges_copied, 1)
            dve.wait_ge(qrow, 1)
            dve.tensor_copy(qtab[0:1, :, :].rearrange("o q m -> o m q"),
                            ps_b[0:1, 0:4 * QH].rearrange("o (m q) -> o m q", m=2)).then_inc(qtab_ready, 1)

            for g in range(NG):
                s = g % 2
                if g < NG - 1:
                    dve.wait_ge(xin_in[s], 16 * (g // 2 + 1))
                else:
                    dve.wait_ge(xin_in[s], 16 * (g // 2 + 2))
                x_g = xin[s][:, :].rearrange("p (b d) -> p b d", d=D)
                xn_g = xn[s][:, :].rearrange("p (b d) -> p b d", d=D)
                for b in range(XG):
                    dve.bn_stats(bn1[:, b * 6:(b + 1) * 6], x_g[:, b, :])
                dve.drain()
                for b in range(XG):
                    dve.bn_aggr(mv1[:, 2 * b:2 * b + 2], bn1[:, b * 6:(b + 1) * 6])
                dve.drain()
                dve.tensor_scalar(mv1[:, 1:2 * XG:2], mv1[:, 1:2 * XG:2], EPS, None, ALU.add).then_inc(var1_ready, 1)
                dve.tensor_copy(mean1[:, g * XG:(g + 1) * XG], mv1[:, 0:2 * XG:2])
                dve.wait_ge(ln1_ready, g + 1)
                newton(rstd1[:, g * XG:(g + 1) * XG], mv1[:, 1:2 * XG:2], nt1[:, XG:2 * XG], nt1[:, 0:XG])
                dve.drain()
                if g >= 2:
                    dve.wait_ge(hi_copied, g - 1)
                    dve.wait_ge(low_done, g - 1)
                for b in range(XG):
                    c = g * XG + b
                    mm = dve.tensor_scalar(xn_g[:, b, :], x_g[:, b, :], mean1[:, c:c + 1], rstd1[:, c:c + 1],
                                           ALU.subtract, ALU.mult)
                mm.then_inc(xn_ready, 1)
                dve.drain().then_inc(xin_used, 1)
                dve.tensor_tensor(r1[s][:, :], xn[s][:, :],
                                  xn[s][:, :].bitcast(BF16).rearrange("p (d t) -> p d t", t=2)[:, :, 1],
                                  ALU.subtract).then_inc(r1_ready, 1)
            dve.wait_ge(consts, 1)

            def quad_rows(q, k):
                dve.tensor_copy(idx[:, k * TQ:(k + 1) * TQ], src_t[:, ds(q, 1), :]).then_inc(idx_ready, 1)

            def select(q, s, b):
                dve.tensor_scalar(rel[:, s, :], dst_t[:, ds(q, 1), :], block0[:, ds(b, 1)], None, ALU.subtract)
                dve.drain()
                for j in range(TQ):
                    last = dve.tensor_scalar(sel[:, s, j, :], lane[:, :], rel[:, s, j:j + 1], None, ALU.is_equal)
                last.then_inc(sel_ready, 1)

            def add(s, b):
                to = acc[:, ds(b * AW, AW)]
                dve.tensor_tensor(to, to, ps_q[s][:, 0:AW], ALU.add).then_inc(acc_done, 1)

            n = dve.alloc_register("visits")
            b = dve.alloc_register("visit_block")
            pending = dve.alloc_register("pending_block")
            regs = [dve.alloc_register(f"quad_blocks{i}") for i in range(2 * QS)]
            dve.reg_mov(n, 0)
            dve.reg_mov(pending, 0)
            for q in range(3):
                quad_rows(q, q)
            dve.drain()
            with dve.Fori(0, NQ // QS) as u:
                dve.load(regs, qtab[0:1, ds(u * QS, QS), :])
                for k in range(QS):
                    q = u * QS + k
                    dve.reg_mov(b, regs[2 * k])
                    with dve.While(lambda: dve.snap(b) < dve.snap(regs[2 * k + 1])):
                        dve.wait_ge(visit_done, dve.snap(n) + 2)
                        select(q, (k + 1) % 2, dve.snap(b, min_val=0, max_val=NB - 1))
                        add((k + 1) % 2, dve.snap(pending, min_val=0, max_val=NB - 1))
                        dve.reg_mov(pending, b)
                        dve.reg_add(n, n, 1)
                        dve.reg_add(b, b, 1)
                    dve.wait_ge(visit_done, dve.snap(n) + 1)
                    select(q, k % 2, dve.snap(b, min_val=0, max_val=NB - 1))
                    dve.wait_ge(visit_done, dve.snap(n) + 2)
                    add((k + 1) % 2, dve.snap(pending, min_val=0, max_val=NB - 1))
                    dve.reg_mov(pending, b)
                    dve.reg_add(n, n, 1)
                    quad_rows(q + 3, (k + 3) % QS)
            dve.drain()
            dve.wait_ge(visit_done, dve.snap(n) + 2)
            add((NQ - 1) % 2, dve.snap(pending, min_val=0, max_val=NB - 1))
            dve.drain().then_inc(acc_clear, 1)
            dve.sem_inc(xb_free, 1)
            dve.sem_inc(crow_free, 1)
            dve.wait_ge(const_in, 16 * 4)

            def node(i, rows):
                c = i
                one = ds(c, 1)
                dve.wait_ge(xb_in, 16 * (i + 1))
                dve.tensor_scalar(cat[:, 0:D], xb[:, :], mean1[:, one], rstd1[:, one], ALU.subtract, ALU.mult)
                dve.tensor_scalar(sm[:, 20:21], acc[:, ds(c * AW + D, 1)], 1.0, None, ALU.max)
                dve.drain()
                dve.reciprocal(sm[:, 21:22], sm[:, 20:21])
                dve.drain()
                dve.tensor_scalar(cat[:, D:2 * D], acc[:, ds(c * AW, D)], sm[:, 21:22], None,
                                  ALU.mult).then_inc(cat_ready, 1)
                dve.wait_ge(zln_ready, i + 1)
                newton(sm[:, 4:5], sm[:, 0:1], sm[:, 2:3], sm[:, 3:4])
                dve.drain()
                dve.wait_ge(row_free, i + 1)
                dve.scalar_tensor_tensor(out=row[:, 0:D], in0=ps_b[:, 0:D], scalar=sm[:, 4:5], in1=xb[:, :],
                                         op0=ALU.mult, op1=ALU.add).then_inc(xb_free, 1)
                dve.drain()
                dve.tensor_tensor(row[:, 0:D], row[:, 0:D], gb_sb[:, :], ALU.add).then_inc(x1_ready, 1)
                dve.drain()
                dve.bn_stats(bn[:, :], row[:, 0:D])
                dve.drain()
                dve.bn_aggr(sm[:, 8:10], bn[:, :])
                dve.drain()
                dve.tensor_scalar(sm[:, 10:11], sm[:, 9:10], EPS, None, ALU.add).then_inc(var2_ready, 1)
                dve.tensor_copy(row[:, C_MEAN:C_MEAN + 1], sm[:, 8:9])
                dve.tensor_copy(row[:, C_NODE:C_NODE + 1], node_id[:, one])
                dve.wait_ge(ln2_ready, i + 1)
                newton(row[:, C_RSTD:C_RSTD + 1], sm[:, 10:11], sm[:, 12:13], sm[:, 13:14])
                dve.drain()
                dve.tensor_scalar(cat[:, D:2 * D], row[:, 0:D], row[:, C_MEAN:C_MEAN + 1],
                                  row[:, C_RSTD:C_RSTD + 1], ALU.subtract, ALU.mult).then_inc(xl_ready, 1)
                dve.wait_ge(logit_ps, i + 1)
                dve.tensor_tensor(g8[:, 0, :], ps_b[:, D:D + EX], gateb_sb[:, :], ALU.add)
                dve.drain()
                dve.tensor_reduce(sm[:, 16:17], g8[:, 0, :], AX, ALU.max, negate=True).then_inc(logit_ready, 1)
                dve.wait_ge(exp_ready, i + 1)
                dve.reciprocal(sm[:, 18:19], sm[:, 17:18])
                dve.drain()
                dve.tensor_scalar(g8[:, 2, :], g8[:, 1, :], sm[:, 18:19], None, ALU.mult)
                dve.drain()
                dve.tensor_reduce(row[:, C_GATE:C_GATE + 1], g8[:, 2, :], AX, ALU.max)
                dve.drain()
                dve.scalar_tensor_tensor(out=g8[:, 3, :], in0=g8[:, 2, :], scalar=row[:, C_GATE:C_GATE + 1],
                                         in1=rev[:, :], op0=ALU.is_equal, op1=ALU.mult)
                dve.drain()
                dve.tensor_reduce(sm[:, 19:20], g8[:, 3, :], AX, ALU.max)
                dve.drain()
                dve.tensor_scalar(hot[:, :], rev[:, :], sm[:, 19:20], None, ALU.is_equal).then_inc(hot_ready, 1)
                dve.wait_ge(count_ps, i + 1)
                dve.tensor_tensor(g8[:, 6, :], ps_b[:, D + EX:D + 2 * EX], seen[:, :], ALU.add)
                dve.drain()
                dve.tensor_tensor(g8[:, 6, :], g8[:, 6, :], hot[:, :], ALU.mult)
                dve.tensor_tensor(seen[:, :], ps_b[:, D + 2 * EX:D + 3 * EX], seen[:, :], ALU.add)
                dve.drain()
                dve.tensor_reduce(sm[:, 22:23], g8[:, 6, :], AX, ALU.max)
                dve.drain()
                dve.tensor_scalar(sm[:, 23:24], sm[:, 22:23], float(CAP), float(EX * SLOTS), ALU.is_gt, ALU.mult)
                dve.tensor_scalar(sm[:, 24:25], sm[:, 19:20], float(-SLOTS), float(EX * SLOTS - 1), ALU.mult, ALU.add)
                dve.drain()
                dve.tensor_tensor(sm[:, 22:23], sm[:, 22:23], sm[:, 23:24], ALU.add)
                dve.drain()
                dve.tensor_tensor(slot[:, :], sm[:, 22:23], sm[:, 24:25], ALU.add).then_inc(row_ready, 1)

            with dve.Fori(0, NB - 1) as i:
                node(i, P)
            node(NB - 1, LAST)

            with dve.Fori(0, EX) as e:
                with dve.Fori(0, CH) as c:
                    i = e * CH + c
                    dve.wait_ge(crow_in, 32 * (i + 1))
                    dve.tensor_scalar(hid[:, 0:D], crow[:, 0:D], crow[:, C_MEAN:C_MEAN + 1],
                                      crow[:, C_RSTD:C_RSTD + 1], ALU.subtract, ALU.mult).then_inc(xc_ready, 1)
                    dve.wait_ge(hid_ps, 2 * i + 1)
                    dve.tensor_copy(hid[:, 0:512], ps_h[:, 0:512]).then_inc(hid_ready, 1)
                    dve.wait_ge(y_ready, i + 1)
                    y, keep, lim = hid[:, 0:D], hid[:, 2 * D:3 * D], res
                    dve.tensor_tensor(y, ps_b[:, 0:D], b2_b[:, :], ALU.add)
                    dve.drain()
                    dve.tensor_scalar(y, y, crow[:, C_GATE:C_GATE + 1], None, ALU.mult)
                    dve.drain()
                    dve.tensor_scalar(lim, y, -1e4, 1e4, ALU.max, ALU.min)
                    dve.tensor_tensor(keep, y, y, ALU.is_equal)
                    dve.drain()
                    dve.tensor_tensor(lim, lim, keep, ALU.mult)
                    dve.drain()
                    dve.tensor_scalar(keep.bitcast(I32), y, 0.0, 0.0, ALU.mult, ALU.is_equal)
                    dve.drain()
                    dve.copy_predicated(lim, keep.bitcast(I32), y)
                    dve.tensor_copy(node_i[:, :], crow[:, C_NODE:C_NODE + 1])
                    dve.drain()
                    dve.tensor_tensor(lim, lim, crow[:, 0:D], ALU.add).then_inc(res_ready, 1)


_INS = ["x", "src", "dst", "L0_gnn_weight", "L0_gnn_bias", "L0_ffn_gate_w", "L0_ffn_gate_b",
        "L0_ffn_w1", "L0_ffn_b1", "L0_ffn_w2", "L0_ffn_b2"]


def kernel(**inputs):
    import concourse.bacc as _bacc
    from concourse.bass_utils import run_bass_kernel_spmd as _run

    nc = _bacc.Bacc("TRN2", target_bir_lowering=False, num_devices=1, dynamic_dma_scratch_size=4096)
    arrays, args = {}, []
    for name in _INS:
        a = np.ascontiguousarray(inputs[name])
        arrays[f"in_{name}"] = a
        args.append(nc.dram_tensor(f"in_{name}", a.shape, mybir.dt.from_np(a.dtype), kind="ExternalInput").ap())
    args.append(nc.dram_tensor("out_0", (N, D), FP32, kind="ExternalOutput").ap())
    gnn_moe_layer(nc, *args)
    r = _run(nc, [arrays], core_ids=[0])
    return r.results[0]["out_0"]
```

```python
import numpy as np
import concourse.bass as bass
from concourse import mybir
from contextlib import ExitStack

FP32 = mybir.dt.float32
BF16 = mybir.dt.bfloat16
I32 = mybir.dt.int32
I16 = mybir.dt.int16
ALU = mybir.AluOpType
ACT = mybir.ActivationFunctionType
AX = mybir.AxisListType.X

P = 128
N = 6250
D = 256
E_EDGES = 100000
NB = -(-N // P)
LAST = N - (NB - 1) * P
TQ = 4
QE = TQ * P
QH = 98
NQ = 2 * QH
QS = 4
FULLQ = E_EDGES // QE
TAIL = E_EDGES - FULLQ * QE
PAD_DST = 16383
NPART = 3
XG = 7
NG = NB // XG
EX = 8
F = 1024
JF = F // P
KD = D // P
CAP = -(-5 * N // (4 * EX))
CH = -(-CAP // P)
SLOTS = CH * P
ROW = 260
C_MEAN, C_RSTD, C_GATE, C_NODE = D, D + 1, D + 2, D + 3
EPS = 1e-5
AW = D + 1
TRIPS = NQ // QS
C0 = 6
TABW = 2 * TRIPS + 6
NSLOTS = 2 * TRIPS + EX * CH + 6
RV = EX + 1
DISP_ROWS = EX * SLOTS + P
FAR = 1 << 20


def gnn_moe_layer(nc, x, src, dst, gnn_w, gnn_b, gate_w, gate_b, w1, b1, w2, b2, out):
    ds = bass.ds
    parts_d = nc.dram_tensor("parts_d", (N, NPART * D), BF16, kind="Internal").ap()
    disp_d = nc.dram_tensor("disp_d", (DISP_ROWS, ROW), FP32, kind="Internal").ap()

    ctx = ExitStack()
    with ctx:
        def sb(name, shape, dt):
            return ctx.enter_context(nc.sbuf_tensor(name, shape, dt))

        def pb(name, shape):
            return ctx.enter_context(nc.psum_tensor(name, shape, FP32))

        def sem(name):
            return ctx.enter_context(nc.semaphore(name))

        w1_sb = sb("w1_sb", [P, KD, EX * F], FP32)
        w2_sb = sb("w2_sb", [P, JF, EX * D], FP32)
        acc = sb("acc", [P, NB * AW], FP32)
        ring = sb("ring", [P, 2 * TQ, NPART * D], BF16)
        dst_t = sb("dst_t", [P, NQ, TQ], I16)
        src_t = sb("src_t", [P, NQ + 3, TQ], I16)
        idx = sb("idx", [P, QS * TQ], I32)
        rel = sb("rel", [P, 2, TQ], FP32)
        sel = sb("sel", [P, 2, TQ, P], BF16)
        ident = sb("ident", [P, P], FP32)
        tri = sb("tri", [P, P], BF16)
        ones = sb("ones", [P, P], BF16)
        ones_bf = sb("ones_bf", [P, 1], BF16)
        lane = sb("lane", [P, P], BF16)
        block0 = sb("block0", [P, NB], FP32)
        node_id = sb("node_id", [P, NB], FP32)
        rev = sb("rev", [P, EX], FP32)
        rev9 = sb("rev9", [P, EX], FP32)
        mean1 = sb("mean1", [P, NB], FP32)
        rstd1 = sb("rstd1", [P, NB], FP32)
        gw_sb = sb("gw_sb", [P, 2 * KD, D], FP32)
        gb_sb = sb("gb_sb", [P, D], FP32)
        gatew_sb = sb("gatew_sb", [P, KD, EX], FP32)
        gateb_sb = sb("gateb_sb", [P, EX], FP32)
        b1_t = sb("b1_t", [P, EX * JF], FP32)
        qtab = sb("qtab", [1, NQ, 2], I16)
        ntab = sb("ntab", [1, TABW], I16)
        valid = sb("valid", [P, TABW], FP32)
        ctab = sb("ctab", [1, NSLOTS, 2], I16)
        ends = sb("ends", [1, 2], I16)
        last_f = sb("last_f", [1, 1], FP32)
        seen = sb("seen", [P, EX], FP32)
        taken = sb("taken", [1, EX], FP32)
        xb = sb("xb", [P, D], FP32)
        cat = sb("cat", [P, 2 * D], FP32)
        cat_t = sb("cat_t", [P, 2 * KD, P], FP32)
        row = sb("row", [P, ROW], FP32)
        slot = sb("slot", [P, 1], I32)
        left_i = sb("left_i", [1, EX], I32)
        sm = sb("sm", [P, 32], FP32)
        g8 = sb("g8", [P, 8, EX], FP32)
        hot = sb("hot", [P, EX], BF16)
        bn = sb("bn", [P, 6], FP32)
        xs = sb("xs", [P, ROW], FP32)
        ys = sb("ys", [P, ROW], FP32)
        b2_b = sb("b2_b", [P, D], FP32)
        hid = sb("hid", [P, F], FP32)
        hid_t = sb("hid_t", [P, JF, P], FP32)
        xc_t = hid_t[:, 0:KD, :]
        res = hid[:, D:2 * D]
        node_i = sb("node_i", [P, 1], I32)

        w1_flat = w1_sb[:, :, :].rearrange("p k f -> p (k f)")
        w2_flat = w2_sb[:, :, :].rearrange("p j f -> p (j f)")

        def carve(flat, at, n):
            return flat[:, at:at + n]

        XW = XG * D
        xin = [carve(w1_flat, s * XW, XW) for s in range(2)]
        xn = [carve(w1_flat, (2 + s) * XW, XW) for s in range(2)]
        r1 = [carve(w1_flat, (4 + s) * XW, XW) for s in range(2)]
        parts = [carve(w2_flat, s * NPART * XW // 2, NPART * XW // 2).bitcast(BF16) for s in range(2)]
        at = NPART * XW
        dst_i = carve(w2_flat, at, 2 * QE).bitcast(I32)
        src_i = carve(w2_flat, at + 2 * QE, 2 * QE).bitcast(I32)
        dst_f = carve(w2_flat, at + 4 * QE, 2 * QE)
        src_f = carve(w2_flat, at + 6 * QE, 2 * QE)
        dst_m = carve(w2_flat, at + 8 * QE, 2 * QE)
        b1_r = w1_flat[0:EX * JF, 6 * XW:6 * XW + P]
        qmm = carve(w2_flat, at + 10 * QE, 4)
        qmi = carve(w2_flat, at + 10 * QE + 8, 4).bitcast(I32)
        qmf = carve(w2_flat, at + 10 * QE + 16, 4)
        bn1 = carve(w1_flat, 6 * XW + P, XG * 6)
        mv1 = carve(w1_flat, 6 * XW + P + 64, XG * 4)
        nt1 = carve(w1_flat, 6 * XW + P + 128, XG * 4)
        tabs = [carve(w2_flat, at + 10 * QE + 32 + i * 2 * TABW, 2 * TABW)[0:1, :] for i in range(4)]
        one_row = carve(w2_flat, at + 10 * QE + 32 + 8 * TABW, P)[0:1, :]

        ps_q = [pb(f"ps_q{i}", [P, 512]) for i in range(2)]
        ps_a = pb("ps_a", [P, 4, P])
        ps_b = pb("ps_b", [P, 512])
        ps_h = pb("ps_h", [P, F])
        ps_t = pb("ps_t", [P, JF, P])

        stage_clear = sem("stage_clear")
        stage_in = sem("stage_in")
        const_in = sem("const_in")
        b1_in = sem("b1_in")
        consts = sem("consts")
        pool_step = sem("pool_step")
        pool_turn = sem("pool_turn")
        sp_turn = sem("sp_turn")
        xin_in = [sem(f"xin_in{s}") for s in range(2)]
        xin_used = sem("xin_used")
        var1_ready = sem("var1_ready")
        ln1_ready = sem("ln1_ready")
        xn_ready = sem("xn_ready")
        r1_ready = sem("r1_ready")
        hi_copied = sem("hi_copied")
        low_done = sem("low_done")
        parts_out = [sem(f"parts_out{s}") for s in range(2)]
        stage_f = sem("stage_f")
        edges_t = sem("edges_t")
        edges_copied = sem("edges_copied")
        qblocks = sem("qblocks")
        qrow = sem("qrow")
        qtab_ready = sem("qtab_ready")
        acc_clear = sem("acc_clear")
        weights_in = sem("weights_in")
        disp_clear = sem("disp_clear")
        idx_ready = sem("idx_ready")
        gathered = [sem(f"gathered{s}") for s in range(4)]
        ring_free = sem("ring_free")
        sel_ready = sem("sel_ready")
        visit_done = sem("visit_done")
        acc_done = sem("acc_done")
        vrow = sem("vrow")
        valid_ps = sem("valid_ps")
        valid_ready = sem("valid_ready")
        xb_in = sem("xb_in")
        xb_free = sem("xb_free")
        cat_ready = sem("cat_ready")
        cat_ps = sem("cat_ps")
        catt_ready = sem("catt_ready")
        z_ready = sem("z_ready")
        zln_ready = sem("zln_ready")
        x1_ready = sem("x1_ready")
        var2_ready = sem("var2_ready")
        ln2_ready = sem("ln2_ready")
        xl_ready = sem("xl_ready")
        xl_ps = sem("xl_ps")
        xlt_ready = sem("xlt_ready")
        logit_ps = sem("logit_ps")
        logit_ready = sem("logit_ready")
        exp_ready = sem("exp_ready")
        hot_ready = sem("hot_ready")
        count_ps = sem("count_ps")
        row_ready = sem("row_ready")
        x1_out = sem("x1_out")
        disp_out = sem("disp_out")
        code_ready = sem("code_ready")
        ends_ready = sem("ends_ready")
        xs_in = sem("xs_in")
        ys_in = sem("ys_in")
        xc_ready = sem("xc_ready")
        xc_ps = sem("xc_ps")
        xct_ready = sem("xct_ready")
        hid_ps = sem("hid_ps")
        hid_ready = sem("hid_ready")
        hidt_ps = sem("hidt_ps")
        hidt_ready = sem("hidt_ready")
        y_ready = sem("y_ready")
        res_ready = sem("res_ready")
        res_out = sem("res_out")

        block = ctx.enter_context(nc.Block())

        def chunks(t):
            return t - (C0 - 1)

        @block.sync
        def _(sp):
            def load_x(g, s, blocks):
                sp.dma_start(xin[s][:, 0:blocks * D].rearrange("p (b d) -> p b d", d=D),
                             x[ds(g * (XG * P), blocks * P), :].rearrange("(b p) d -> p b d", p=P)
                             ).then_inc(xin_in[s], 16)

            def store_parts(g, s, blocks):
                sp.dma_start(parts_d[ds(g * (XG * P), blocks * P), :].rearrange("(b p) d -> p b d", p=P),
                             parts[s][:, 0:blocks * NPART * D].rearrange("p (b d) -> p b d", d=NPART * D)
                             ).then_inc(parts_out[s], 16)

            load_x(0, 0, XG)
            load_x(1, 1, XG)
            sp.wait_ge(stage_clear, 1)
            for dram, staged in ((dst, dst_i), (src, src_i)):
                sp.dma_start(staged[0:QH, 0:QE],
                             dram[0:QH * QE].rearrange("(p e) -> p e", e=QE)).then_inc(stage_in, 16)
                sp.dma_start(staged[0:FULLQ - QH, QE:2 * QE],
                             dram[QH * QE:FULLQ * QE].rearrange("(p e) -> p e", e=QE)).then_inc(stage_in, 16)
                sp.dma_start(staged[FULLQ - QH:FULLQ - QH + 1, QE:QE + TAIL],
                             dram[FULLQ * QE:E_EDGES].rearrange("(p e) -> p e", p=1)).then_inc(stage_in, 16)
            sp.dma_start(b1_r, b1.rearrange("e (j p) -> (e j) p", p=P)).then_inc(b1_in, 16)

            for g in range(NG):
                s = g % 2
                sp.wait_ge(low_done, g + 1)
                sp.wait_ge(hi_copied, g + 1)
                if g < NG - 1:
                    store_parts(g, s, XG)
                else:
                    store_parts(g, s, XG - 1)
                    sp.dma_start(parts_d[(NB - 1) * P:N, :],
                                 parts[s][0:LAST, (XG - 1) * NPART * D:XG * NPART * D]).then_inc(parts_out[s], 16)
                if g + 2 < NG:
                    sp.wait_ge(xin_used, g + 1)
                    load_x(g + 2, s, XG if g + 2 < NG - 1 else XG - 1)
                    if g + 2 == NG - 1:
                        sp.dma_start(xin[s][0:LAST, (XG - 1) * D:XG * D], x[(NB - 1) * P:N, :]
                                     ).then_inc(xin_in[s], 16)
            sp.wait_ge(parts_out[0], 16 * (NG // 2 + 2))
            sp.wait_ge(parts_out[1], 16 * (NG // 2))
            sp.wait_ge(valid_ready, 1)
            sp.wait_ge(edges_copied, 5)
            for k in range(KD):
                sp.dma_start(w1_sb[:, k, :].rearrange("p (e f) -> p e f", f=F),
                             w1[:, k * P:(k + 1) * P, :].rearrange("e p f -> p e f")).then_inc(weights_in, 16)
            for j in range(JF):
                sp.dma_start(w2_sb[:, j, :].rearrange("p (e f) -> p e f", f=D),
                             w2[:, j * P:(j + 1) * P, :].rearrange("e p f -> p e f")).then_inc(weights_in, 16)

            sp.wait_ge(consts, 1)
            sp.dma_start(disp_d.rearrange("(t p) c -> p t c", p=P),
                         row[:, :].rearrange("p (a c) -> p a c", a=1).to_broadcast((P, DISP_ROWS // P, ROW))
                         ).then_inc(x1_out, 16)

            blk, blk2 = sp.alloc_register("node_block"), sp.alloc_register("next_node_block")
            code = [sp.alloc_register(n) for n in ("chunk_row", "chunk_expert")]
            last, end, t_reg = (sp.alloc_register(n) for n in ("last_node_slot", "chunk_end", "slot"))

            def next_block(t, known):
                if known is None:
                    sp.load([blk2], ntab[0:1, ds(t, 1)])
                    return sp.snap(sp.snap(blk2, min_val=0, max_val=NB - 2) * P)
                return known * P

            def load_node(t, known=None, rows=P):
                b = next_block(t, known)
                if not isinstance(t, int):
                    sp.wait_ge(xb_free, t)
                sp.dma_start(xb[0:rows, :], x[ds(b, rows), :]).then_inc(xb_in, 16)

            def load_xs(t):
                sp.sem_inc(sp_turn, 1)
                sp.load(code, ctab[0:1, ds(t, 1), :])
                sp.dma_start(xs[:, :], disp_d[ds(sp.snap(code[0], min_val=0, max_val=EX * SLOTS), P), :]
                             ).then_inc(xs_in, 16)

            def trip(t, node=True, chunk=True, known=None, rows=P, next_known=None, next_rows=P, next_node=True):
                if chunk:
                    sp.load(code, ctab[0:1, ds(t, 1), :])
                    first = sp.snap(code[0], min_val=0, max_val=EX * SLOTS)
                    e = sp.snap(code[1], min_val=0, max_val=EX - 1)
                    sp.wait_ge(res_ready, chunks(t))
                    sp.dma_start(ys[:, :], disp_d[ds(first, P), :]).then_inc(ys_in, 16)
                    sp.dma_start(b2_b[:, :], b2[ds(e, 1), :].to_broadcast((P, D))).then_inc(ys_in, 16)
                if node:
                    if known is None:
                        sp.load([blk], ntab[0:1, ds(t, 1)])
                    b = sp.snap(sp.snap(blk, min_val=0, max_val=NB - 2) * P) if known is None else known * P
                    sp.wait_ge(x1_ready, t + 1)
                    sp.dma_start(out[ds(b, rows), :], row[0:rows, 0:D]).then_inc(x1_out, 16)
                    if next_node:
                        load_node(t + 1, next_known, next_rows)
                if chunk:
                    sp.wait_ge(code_ready, chunks(t))
                    sp.wait_ge(xc_ready, chunks(t))
                    if node:
                        sp.sem_inc(sp_turn, 1)
                        sp.wait_ge(disp_out, 16 * t)
                        sp.wait_ge(x1_out, 16 * t)
                    load_xs(t + 1)

            sp.wait_ge(qtab_ready, 2)
            sp.wait_ge(x1_out, 16)
            sp.sem_inc(sp_turn, 1)
            load_node(0)
            with sp.Fori(0, C0) as t:
                trip(t, chunk=False)
            load_xs(C0)
            with sp.Fori(C0, TRIPS) as t:
                trip(t)
            sp.load([last], ends[0:1, 0:1])
            sp.reg_mov(t_reg, TRIPS)
            with sp.While(lambda: sp.snap(t_reg) + 1 < sp.snap(last)):
                trip(sp.snap(t_reg, min_val=TRIPS, max_val=TABW - 4))
                sp.reg_add(t_reg, t_reg, 1)
            trip(sp.snap(t_reg, min_val=TRIPS, max_val=TABW - 4), next_known=NB - 1, next_rows=LAST)
            sp.reg_add(t_reg, t_reg, 1)
            trip(sp.snap(t_reg, min_val=TRIPS, max_val=TABW - 3), known=NB - 1, rows=LAST, next_node=False)
            sp.reg_add(t_reg, t_reg, 1)
            sp.wait_ge(disp_out, 16 * (sp.snap(t_reg) + 1))
            sp.wait_ge(x1_out, 16 * (sp.snap(t_reg) + 1))
            sp.wait_ge(ends_ready, 1)
            sp.sem_inc(sp_turn, 1)
            sp.load([end], ends[0:1, 1:2])
            with sp.While(lambda: sp.snap(t_reg) < sp.snap(end)):
                trip(sp.snap(t_reg, min_val=TRIPS, max_val=NSLOTS - 3), node=False)
                sp.reg_add(t_reg, t_reg, 1)
            sp.wait_ge(ys_in, 32 * (sp.snap(t_reg) - C0))
            sp.wait_ge(xs_in, 16 * (sp.snap(t_reg) - C0 + 1))
            sp.sem_inc(sp_turn, 1)

        @block.gpsimd
        def _(pool):
            pool.memset(dst_i[:, :], PAD_DST)
            pool.memset(src_i[:, :], 0).then_inc(stage_clear, 1)
            pool.memset(ident[:, :], 0.0)
            pool.memset(tri[:, :], 1.0)
            pool.memset(ones[:, :], 1.0)
            pool.memset(seen[:, :], 0.0)
            pool.memset(taken[:, :], 0.0)
            pool.memset(one_row[:, :], 1.0)
            pool.memset(ctab[:, :, 0:1], EX * SLOTS)
            pool.memset(ctab[:, :, 1:2], EX - 1)
            pool.memset(hid[:, :], 0.0)
            pool.memset(hot[:, :], 0.0)
            pool.memset(sm[:, :], 0.0)
            pool.memset(node_i[:, :], FAR)
            pool.memset(row[:, 0:C_NODE], 0.0)
            pool.memset(row[:, C_NODE:C_NODE + 1], float(FAR))
            pool.memset(xb[:, :], 0.0)
            pool.memset(ones_bf[:, :], 1.0).then_inc(pool_step, 1)
            pool.iota(lane[:, :], [[1, P]], base=0, channel_multiplier=0, allow_small_or_imprecise_dtypes=True)
            pool.iota(block0[:, :], [[P, NB]], base=0, channel_multiplier=0, allow_small_or_imprecise_dtypes=True)
            pool.iota(node_id[:, :], [[P, NB]], base=0, channel_multiplier=1, allow_small_or_imprecise_dtypes=True)
            pool.iota(rev[:, :], [[-1, EX]], base=EX, channel_multiplier=0, allow_small_or_imprecise_dtypes=True)
            pool.iota(rev9[:, :], [[-1, EX]], base=EX + RV, channel_multiplier=0,
                      allow_small_or_imprecise_dtypes=True)
            pool.iota(tabs[0][:, 0:2 * TABW], [[1, 2 * TABW]], base=0, channel_multiplier=0,
                      allow_small_or_imprecise_dtypes=True)
            pool.wait_ge(pool_step, 1)
            pool.affine_select(out=ident[:, :], in_=ident[:, :], compare_op=ALU.not_equal, fill=1.0,
                               base=0, pattern=[[-1, P]], channel_multiplier=1)
            pool.affine_select(out=tri[:, :], in_=tri[:, :], compare_op=ALU.is_ge, fill=0.0,
                               base=0, pattern=[[1, P]], channel_multiplier=-1).then_inc(consts, 1)
            for view, dram in ((gb_sb[:, :], gnn_b.rearrange("(a n) -> a n", a=1).to_broadcast((P, D))),
                               (gateb_sb[:, :], gate_b.rearrange("(a n) -> a n", a=1).to_broadcast((P, EX))),
                               (gw_sb[:, :, :], gnn_w.rearrange("(k p) n -> p k n", p=P)),
                               (gatew_sb[:, :, :], gate_w.rearrange("(k p) n -> p k n", p=P))):
                pool.dma_start(view, dram).then_inc(const_in, 16)
            for g in range(NG):
                s = g % 2
                pool.wait_ge(r1_ready, g + 1)
                if g >= 2:
                    pool.wait_ge(parts_out[s], 16 * (g // 2))
                pool.tensor_tensor(
                    out=parts[s][:, :].rearrange("p (b k d) -> p b k d", k=NPART, d=D)[:, :, 2, :],
                    in0=r1[s][:, :].rearrange("p (b d) -> p b d", d=D),
                    in1=r1[s][:, :].bitcast(BF16).rearrange("p (b d t) -> p b d t", d=D, t=2)[:, :, :, 1],
                    op=ALU.subtract).then_inc(low_done, 1)
            pool.wait_ge(parts_out[0], 16 * (NG // 2 + 2))
            pool.wait_ge(parts_out[1], 16 * (NG // 2))
            last, end, t_reg = (pool.alloc_register(n) for n in ("last_node_slot", "chunk_end", "slot"))

            def gather(t, k, half):
                free = pool.snap((t * QS + k) * TQ + 2 * half + 2)
                turn = pool.snap(t * QS + (k + 1))
                pool.wait_ge(idx_ready, turn)
                pool.wait_ge(ring_free, free)
                pool.sem_inc(pool_turn, 1)
                for j in (2 * half, 2 * half + 1):
                    pool.indirect_dma_start(
                        ring[:, (k % 2) * TQ + j, :], None, parts_d[:, :],
                        bass.IndirectOffsetOnAxis(ap=idx[:, k * TQ + j:k * TQ + j + 1], axis=0)
                    ).then_inc(gathered[(2 * k + half) % 4], 16)

            def dispatch(t, rows=P):
                pool.wait_ge(row_ready, t + 1)
                pool.sem_inc(pool_turn, 1)
                pool.indirect_dma_start(
                    disp_d[:, :], bass.IndirectOffsetOnAxis(ap=slot[0:rows, 0:1], axis=0), row[0:rows, :], None,
                    bounds_check=EX * SLOTS - 1, oob_is_err=False).then_inc(disp_out, 16)

            def results(t):
                pool.wait_ge(res_ready, chunks(t))
                pool.sem_inc(pool_turn, 1)
                pool.indirect_dma_start(
                    out[:, :], bass.IndirectOffsetOnAxis(ap=node_i[:, 0:1], axis=0), res, None,
                    bounds_check=N - 1, oob_is_err=False).then_inc(res_out, 16)

            def trip(t, quads=True, node=True, chunk=True):
                for k in range(QS if quads else 1):
                    for half in range(2):
                        if quads:
                            gather(t, k, half)
                        if k == 0 and half == 0 and chunk:
                            results(t)
                        if k == 0 and half == 1 and node:
                            dispatch(t)

            pool.wait_ge(x1_out, 16)
            with pool.Fori(0, C0) as t:
                trip(t, chunk=False)
            with pool.Fori(C0, TRIPS) as t:
                trip(t)
            pool.load([last], ends[0:1, 0:1])
            pool.reg_mov(t_reg, TRIPS)
            with pool.While(lambda: pool.snap(t_reg) < pool.snap(last)):
                trip(pool.snap(t_reg), quads=False)
                pool.reg_add(t_reg, t_reg, 1)
            trip(pool.snap(t_reg), quads=False)
            pool.reg_add(t_reg, t_reg, 1)
            dispatch(pool.snap(t_reg), LAST)
            pool.wait_ge(ends_ready, 1)
            pool.sem_inc(pool_turn, 1)
            pool.load([end], ends[0:1, 1:2])
            with pool.While(lambda: pool.snap(t_reg) < pool.snap(end)):
                trip(pool.snap(t_reg), quads=False, node=False)
                pool.reg_add(t_reg, t_reg, 1)
            results(pool.snap(t_reg))
            pool.wait_ge(res_out, 16 * (pool.snap(t_reg) - C0 + 1))

        @block.scalar
        def _(act):
            def rsqrt_start(to, of, tmp):
                act.activation(tmp, of, ACT.Ln)
                act.drain()
                return act.activation(to, tmp, ACT.Exp, scale=-0.5)

            act.preload_act_table_set("natural_log_exp_and_others")
            act.wait_ge(consts, 1)
            for g in range(NG):
                s = g % 2
                act.wait_ge(var1_ready, g + 1)
                o = (g % 2) * 2 * XG
                rsqrt_start(nt1[:, o + XG:o + 2 * XG], mv1[:, o + 1:o + 2 * XG:2], nt1[:, o:o + XG]
                            ).then_inc(ln1_ready, 1)
                view = parts[s][:, :].rearrange("p (b k d) -> p b k d", k=NPART, d=D)
                act.wait_ge(xn_ready, g + 1)
                if g >= 2:
                    act.wait_ge(parts_out[s], 16 * (g // 2))
                act.activation(view[:, :, 0, :],
                               xn[s][:, :].bitcast(BF16).rearrange("p (b d t) -> p b d t", d=D, t=2)[:, :, :, 1],
                               ACT.Copy)
                act.wait_ge(r1_ready, g + 1)
                act.activation(view[:, :, 1, :],
                               r1[s][:, :].bitcast(BF16).rearrange("p (b d t) -> p b d t", d=D, t=2)[:, :, :, 1],
                               ACT.Copy).then_inc(hi_copied, 1)

            code = [act.alloc_register(n) for n in ("chunk_row", "chunk_expert")]
            last, end, t_reg = (act.alloc_register(n) for n in ("last_node_slot", "chunk_end", "slot"))

            def trip(t, node=True, chunk=True):
                c = chunks(t)
                if node:
                    act.wait_ge(cat_ps, t + 1)
                    act.activation(cat_t[:, :, :], ps_a[:, :, :], ACT.Copy).then_inc(catt_ready, 1)
                if chunk:
                    act.wait_ge(xc_ps, c)
                    act.activation(xc_t, ps_t[:, 0:KD, :], ACT.Copy).then_inc(xct_ready, 1)
                    act.load(code, ctab[0:1, ds(t, 1), :])
                    e = act.snap(code[1], min_val=0, max_val=EX - 1)
                if node:
                    act.wait_ge(z_ready, t + 1)
                    act.activation(cat[:, 0:D], ps_b[:, 0:D], ACT.Square, accum_out=sm[:, 0:1])
                    act.drain()
                    rsqrt_start(sm[:, 2:3], sm[:, 0:1], sm[:, 1:2]).then_inc(zln_ready, 1)
                if chunk:
                    act.wait_ge(hid_ps, 2 * c)
                    act.wait_ge(res_ready, c)
                    act.activation(hid[:, 512:F], ps_h[:, 512:F], ACT.Copy).then_inc(hid_ready, 1)
                if node:
                    act.wait_ge(var2_ready, t + 1)
                    rsqrt_start(sm[:, 12:13], sm[:, 10:11], sm[:, 11:12]).then_inc(ln2_ready, 1)
                if chunk:
                    for h in range(2):
                        act.wait_ge(hidt_ps, 2 * c - 1 + h)
                        for j in range(h * 4, h * 4 + 4):
                            done = act.activation(hid_t[:, j, :], ps_t[:, j, :], ACT.Relu,
                                                  bias=b1_t[:, ds(e * JF + j, 1)])
                        done.then_inc(hidt_ready, 1)
                if node:
                    act.wait_ge(xl_ps, t + 1)
                    act.activation(cat_t[:, 0:KD, :], ps_a[:, 0:KD, :], ACT.Copy).then_inc(xlt_ready, 1)
                    act.wait_ge(logit_ready, t + 1)
                    act.activation(g8[:, 1, :], g8[:, 0, :], ACT.Exp, bias=sm[:, 16:17],
                                   accum_out=sm[:, 17:18]).then_inc(exp_ready, 1)

            with act.Fori(0, C0) as t:
                trip(t, chunk=False)
            with act.Fori(C0, TRIPS) as t:
                trip(t)
            act.load([last], ends[0:1, 0:1])
            act.reg_mov(t_reg, TRIPS)
            with act.While(lambda: act.snap(t_reg) < act.snap(last) + 1):
                trip(act.snap(t_reg, min_val=0, max_val=TABW - 1))
                act.reg_add(t_reg, t_reg, 1)
            act.wait_ge(ends_ready, 1)
            act.load([end], ends[0:1, 1:2])
            with act.While(lambda: act.snap(t_reg) < act.snap(end)):
                trip(act.snap(t_reg, min_val=0, max_val=NSLOTS - 1), node=False)
                act.reg_add(t_reg, t_reg, 1)

        @block.tensor
        def _(pe):
            pe.sem_inc(ring_free, 2 * TQ)
            pe.sem_inc(count_ps, 1)
            pe.sem_inc(visit_done, 2)
            pe.wait_ge(consts, 1)
            pe.wait_ge(stage_f, 1)
            for m, staged in enumerate((dst_f, src_f)):
                for h in range(2):
                    if m or h:
                        pe.wait_ge(edges_copied, 2 * m + h)
                    for j in range(TQ):
                        last = pe.transpose(ps_a[:, j, 0:QH], staged[0:QH, h * QE + j * P:h * QE + (j + 1) * P],
                                            ident[0:QH, 0:QH])
                    last.then_inc(edges_t, 1)
            pe.wait_ge(b1_in, 16)
            pe.wait_ge(edges_copied, 4)
            pe.transpose(ps_a[:, 0, 0:EX * JF], b1_r, ident[0:EX * JF, 0:EX * JF]).then_inc(edges_t, 1)
            pe.wait_ge(qblocks, 1)
            for m in range(4):
                last = pe.matmul(ps_b[0:1, m * QH:(m + 1) * QH], qmf[0:QH, m:m + 1], ident[0:QH, 0:QH],
                                 start=True, stop=True)
            last.then_inc(qrow, 1)

            pe.wait_ge(vrow, 1)
            pe.matmul(ps_b[:, 0:TABW], one_row[:, 0:P], tabs[3][:, 0:TABW], start=True, stop=True
                      ).then_inc(valid_ps, 1)

            n = pe.alloc_register("visits")
            b = pe.alloc_register("visit_block")
            pe.reg_mov(n, 0)
            regs = [pe.alloc_register(f"quad_blocks{i}") for i in range(2 * QS)]
            code = [pe.alloc_register(m) for m in ("chunk_row", "chunk_expert")]
            last, end, t_reg = (pe.alloc_register(m) for m in ("last_node_slot", "chunk_end", "slot"))
            pe.wait_ge(qtab_ready, 2)

            def visit(t, k, s, final, between=()):
                ps = ps_q[s]
                for j in range(TQ):
                    if j % 2 == 0:
                        pe.wait_ge(gathered[(2 * k + j // 2) % 4], 32 * (2 * t + k // 2 + 1))
                    for part in range(NPART):
                        mm = pe.matmul(ps[:, 0:D], sel[:, s, j, :],
                                       ring[:, (k % 2) * TQ + j, part * D:(part + 1) * D],
                                       start=(j == 0 and part == 0), stop=(j == TQ - 1 and part == NPART - 1),
                                       skip_group_check=True)
                    if final:
                        mm.then_inc(ring_free, 1)
                    mm = pe.matmul(ps[:, D:AW], sel[:, s, j, :], ones_bf[:, :], start=False,
                                   stop=(j == TQ - 1), skip_group_check=True)
                    if j == TQ - 1:
                        mm.then_inc(visit_done, 1)
                    if j < len(between):
                        between[j]()

            def quad(t, k, between):
                pe.reg_mov(b, regs[2 * k])
                with pe.While(lambda: pe.snap(b) < pe.snap(regs[2 * k + 1])):
                    pe.wait_ge(sel_ready, pe.snap(n) + 1)
                    pe.wait_ge(acc_done, pe.snap(n) + 2)
                    visit(t, k, (k + 1) % 2, False)
                    pe.reg_add(n, n, 1)
                    pe.reg_add(b, b, 1)
                pe.wait_ge(sel_ready, pe.snap(n) + 1)
                pe.wait_ge(acc_done, pe.snap(n) + 1)
                visit(t, k, k % 2, True, between)
                pe.reg_add(n, n, 1)

            def trip(t, quads=True, node=True, chunk=True, rows=P):
                c = chunks(t)
                if chunk:
                    pe.load(code, ctab[0:1, ds(t, 1), :])
                    e = pe.snap(code[1], min_val=0, max_val=EX - 1)

                def cat_transposes():
                    pe.wait_ge(cat_ready, t + 1)
                    for k in range(2 * KD):
                        last_ = pe.transpose(ps_a[:, k, :], cat[:, k * P:(k + 1) * P], ident[:, :])
                    last_.then_inc(cat_ps, 1)

                def xc_transposes():
                    pe.wait_ge(xc_ready, c)
                    for k in range(KD):
                        last_ = pe.transpose(ps_t[:, k, :], hid[:, k * P:(k + 1) * P], ident[:, :])
                    last_.then_inc(xc_ps, 1)

                def linear(h):
                    if h == 0:
                        if chunk:
                            pe.wait_ge(res_ready, c)
                        pe.wait_ge(catt_ready, t + 1)
                    for k in (2 * h, 2 * h + 1):
                        last_ = pe.matmul(ps_b[:, 0:D], cat_t[:, k, :], gw_sb[:, k, :],
                                          start=(k == 0), stop=(k == 2 * KD - 1))
                    if h == 1:
                        last_.then_inc(z_ready, 1)

                def up(h):
                    if h == 0:
                        if node:
                            pe.wait_ge(row_ready, t + 1)
                        pe.wait_ge(xct_ready, c)
                    for k in range(KD):
                        last_ = pe.matmul(ps_h[:, h * 512:(h + 1) * 512], xc_t[:, k, :],
                                          w1_sb[:, k, ds(e * F + h * 512, 512)],
                                          start=(k == 0), stop=(k == KD - 1))
                    last_.then_inc(hid_ps, 1)

                def hid_transposes(h):
                    if h == 0:
                        pe.wait_ge(hid_ready, 2 * c)
                    for j in range(h * 4, h * 4 + 4):
                        last_ = pe.transpose(ps_t[:, j, :], hid[:, j * P:(j + 1) * P], ident[:, :])
                    last_.then_inc(hidt_ps, 1)

                def down(js):
                    for j in js:
                        if j == 0:
                            if node:
                                pe.wait_ge(x1_ready, t + 1)
                            pe.wait_ge(res_ready, c)
                        if j % 4 == 0:
                            pe.wait_ge(hidt_ready, 2 * c - 1 + j // 4)
                        last_ = pe.matmul(ps_b[:, 0:D], hid_t[:, j, :], w2_sb[:, j, ds(e * D, D)],
                                          start=(j == 0), stop=(j == JF - 1))
                    if js[-1] == JF - 1:
                        last_.then_inc(y_ready, 1)

                def xl_transposes():
                    pe.wait_ge(xl_ready, t + 1)
                    for k in range(KD):
                        last_ = pe.transpose(ps_a[:, k, :], cat[:, D + k * P:D + (k + 1) * P], ident[:, :])
                    last_.then_inc(xl_ps, 1)

                def gate():
                    pe.wait_ge(xlt_ready, t + 1)
                    for k in range(KD):
                        last_ = pe.matmul(ps_a[:, 3, 0:EX], cat_t[:, k, :], gatew_sb[:, k, :],
                                          start=(k == 0), stop=(k == KD - 1))
                    last_.then_inc(logit_ps, 1)

                def counts():
                    pe.wait_ge(hot_ready, t + 1)
                    pe.matmul(ps_h[:, 0:EX], tri[0:rows, :], hot[0:rows, :], start=True, stop=True)
                    pe.matmul(ps_h[:, EX:2 * EX], ones[0:rows, :], hot[0:rows, :],
                              start=True, stop=True).then_inc(count_ps, 1)

                def steps(*parts_):
                    def run():
                        for on, f, *args in parts_:
                            if on:
                                f(*args)
                    return run

                plan = [[steps((node, linear, 0)), steps((node, linear, 1)), steps((chunk, up, 0)),
                         steps((chunk, up, 1))],
                        [steps(), steps((chunk, hid_transposes, 0)), steps((chunk, hid_transposes, 1)),
                         steps((chunk, down, (0, 1)))],
                        [steps((node, xl_transposes)), steps((chunk, down, (2, 3))),
                         steps((node, gate), (chunk, down, (4, 5))), steps((chunk, down, (6, 7)))],
                        []]
                if quads:
                    pe.load(regs, qtab[0:1, ds(t * QS, QS), :])
                if node:
                    cat_transposes()
                if chunk:
                    xc_transposes()
                for k in range(QS):
                    if quads:
                        quad(t, k, plan[k])
                    else:
                        for step in plan[k]:
                            step()
                if node:
                    counts()

            with pe.Fori(0, C0) as t:
                trip(t, chunk=False)
            pe.wait_ge(weights_in, 16 * (KD + JF))
            with pe.Fori(C0, TRIPS) as t:
                trip(t)
            pe.load([last], ends[0:1, 0:1])
            pe.reg_mov(t_reg, TRIPS)
            with pe.While(lambda: pe.snap(t_reg) < pe.snap(last)):
                trip(pe.snap(t_reg, min_val=0, max_val=TABW - 1), quads=False)
                pe.reg_add(t_reg, t_reg, 1)
            trip(pe.snap(t_reg, min_val=0, max_val=TABW - 1), quads=False, rows=LAST)
            pe.reg_add(t_reg, t_reg, 1)
            pe.wait_ge(ends_ready, 1)
            pe.load([end], ends[0:1, 1:2])
            with pe.While(lambda: pe.snap(t_reg) < pe.snap(end)):
                trip(pe.snap(t_reg, min_val=0, max_val=NSLOTS - 1), quads=False, node=False)
                pe.reg_add(t_reg, t_reg, 1)

        @block.vector
        def _(dve):
            def newton(to, v, r, tmp):
                dve.tensor_tensor(tmp, v, r, ALU.mult)
                dve.drain()
                dve.tensor_tensor(tmp, tmp, r, ALU.mult)
                dve.drain()
                dve.tensor_scalar(tmp, tmp, -0.5, 1.5, ALU.mult, ALU.add)
                dve.drain()
                return dve.tensor_tensor(to, tmp, r, ALU.mult)

            dve.sem_inc(acc_done, 1)

            def edge_lists():
                dve.memset(src_t[:, NQ:NQ + 3, :], 0)
                dve.memset(ps_q[1][:, 0:AW], 0.0)
                dve.wait_ge(stage_in, 16 * 6)
                dve.tensor_copy(dst_f[0:QH, :], dst_i[0:QH, :])
                dve.tensor_copy(src_f[0:QH, :], src_i[0:QH, :]).then_inc(stage_f, 1)
                dve.drain()
                dve.scalar_tensor_tensor(out=dst_m[0:QH, :], in0=dst_f[0:QH, :], scalar=float(N), in1=dst_f[0:QH, :],
                                         op0=ALU.is_lt, op1=ALU.mult)
                dve.drain()
                dve.tensor_reduce(qmm[0:QH, 0:2], dst_f[0:QH, :].rearrange("p (h e) -> p h e", h=2), AX, ALU.min)
                dve.tensor_reduce(qmm[0:QH, 2:4], dst_m[0:QH, :].rearrange("p (h e) -> p h e", h=2), AX, ALU.max)
                dve.drain()
                dve.tensor_copy(qmi[0:QH, :], qmm[0:QH, :])
                dve.drain()
                dve.tensor_scalar(qmi[0:QH, :], qmi[0:QH, :], 7, None, ALU.logical_shift_right)
                dve.drain()
                dve.tensor_copy(qmf[0:QH, :], qmi[0:QH, :]).then_inc(qblocks, 1)
                for m, to in enumerate((dst_t, src_t)):
                    for h in range(2):
                        dve.wait_ge(edges_t, 2 * m + h + 1)
                        dve.tensor_copy(to[:, h * QH:(h + 1) * QH, :].rearrange("p q j -> p j q"),
                                        ps_a[:, :, 0:QH]).then_inc(edges_copied, 1)
                dve.wait_ge(edges_t, 5)
                dve.tensor_copy(b1_t[:, :], ps_a[:, 0, 0:EX * JF]).then_inc(edges_copied, 1)
                dve.wait_ge(qrow, 1)
                dve.tensor_copy(qtab[0:1, :, :].rearrange("o q m -> o m q"),
                                ps_b[0:1, 0:4 * QH].rearrange("o (m q) -> o m q", m=2)).then_inc(qtab_ready, 1)

            def slot_tables():
                count, ta, tb, tc = tabs
                dve.memset(ta[:, :], float(NB))
                dve.drain()
                dve.tensor_reduce(ta[:, 0:TRIPS], ps_b[0:1, 0:NQ].rearrange("o (u k) -> o u k", k=QS), AX, ALU.min)
                dve.drain()
                cur, other = ta, tb
                step = 1
                while step < TRIPS:
                    dve.tensor_tensor(other[:, 0:2 * TABW - step], cur[:, 0:2 * TABW - step], cur[:, step:2 * TABW],
                                      ALU.min)
                    dve.tensor_copy(other[:, 2 * TABW - step:2 * TABW], cur[:, 2 * TABW - step:2 * TABW])
                    dve.drain()
                    cur, other = other, cur
                    step *= 2
                dve.memset(tc[:, 0:2], 0.0)
                dve.tensor_copy(tc[:, 2:TABW], cur[:, 1:TABW - 1])
                dve.drain()
                dve.tensor_tensor(ta[:, 0:TABW], tc[:, 0:TABW], count[:, 0:TABW], ALU.subtract)
                dve.drain()
                cur, other = ta, tb
                step = 1
                while step < TABW:
                    dve.tensor_tensor(other[:, step:TABW], cur[:, step:TABW], cur[:, 0:TABW - step], ALU.min)
                    dve.tensor_copy(other[:, 0:step], cur[:, 0:step])
                    dve.drain()
                    cur, other = other, cur
                    step *= 2
                dve.memset(other[:, 0:1], 0.0)
                dve.tensor_tensor(other[:, 1:TABW], cur[:, 0:TABW - 1], count[:, 0:TABW - 1], ALU.add)
                dve.drain()
                dve.tensor_copy(ntab[:, :], other[:, 0:TABW])
                dve.tensor_scalar(last_f[:, :], other[:, TRIPS + 1:TRIPS + 2], -1.0, float(TRIPS + NB), ALU.mult, ALU.add)
                dve.tensor_tensor(tc[:, 0:TABW - 1], other[:, 1:TABW], other[:, 0:TABW - 1], ALU.subtract)
                dve.memset(tc[:, TABW - 1:TABW], 0.0)
                dve.drain().then_inc(vrow, 1)
                dve.tensor_copy(ends[:, 0:1], last_f[:, :]).then_inc(qtab_ready, 1)
                dve.wait_ge(valid_ps, 1)
                dve.tensor_copy(valid[:, :], ps_b[:, 0:TABW])
                dve.drain().then_inc(valid_ready, 1)
                dve.memset(ps_h[:, 0:2 * EX], 0.0)

            def stats(g):
                s = g % 2
                dve.wait_ge(xin_in[s], 16 * (g // 2 + (1 if g < NG - 1 else 2)))
                x_g = xin[s][:, :].rearrange("p (b d) -> p b d", d=D)
                o = s * 2 * XG
                for b in range(XG):
                    dve.bn_stats(bn1[:, b * 6:(b + 1) * 6], x_g[:, b, :])
                dve.drain()
                for b in range(XG):
                    dve.bn_aggr(mv1[:, o + 2 * b:o + 2 * b + 2], bn1[:, b * 6:(b + 1) * 6])
                dve.drain()
                dve.tensor_scalar(mv1[:, o + 1:o + 2 * XG:2], mv1[:, o + 1:o + 2 * XG:2], EPS, None,
                                  ALU.add).then_inc(var1_ready, 1)
                dve.tensor_copy(mean1[:, g * XG:(g + 1) * XG], mv1[:, o:o + 2 * XG:2])

            AC = NB * AW // NG
            stats(0)
            for g in range(NG):
                s = g % 2
                o = s * 2 * XG
                xn_g = xn[s][:, :].rearrange("p (b d) -> p b d", d=D)
                x_g = xin[s][:, :].rearrange("p (b d) -> p b d", d=D)
                if g + 1 < NG:
                    stats(g + 1)
                dve.wait_ge(ln1_ready, g + 1)
                newton(rstd1[:, g * XG:(g + 1) * XG], mv1[:, o + 1:o + 2 * XG:2], nt1[:, o + XG:o + 2 * XG],
                       nt1[:, o:o + XG])
                dve.drain()
                if g >= 2:
                    dve.wait_ge(hi_copied, g - 1)
                    dve.wait_ge(low_done, g - 1)
                for b in range(XG):
                    c = g * XG + b
                    mm = dve.tensor_scalar(xn_g[:, b, :], x_g[:, b, :], mean1[:, c:c + 1], rstd1[:, c:c + 1],
                                           ALU.subtract, ALU.mult)
                mm.then_inc(xn_ready, 1)
                dve.drain().then_inc(xin_used, 1)
                dve.tensor_tensor(r1[s][:, :], xn[s][:, :],
                                  xn[s][:, :].bitcast(BF16).rearrange("p (d t) -> p d t", t=2)[:, :, 1],
                                  ALU.subtract).then_inc(r1_ready, 1)
                if g == 1:
                    edge_lists()
                if g == 2:
                    slot_tables()
                if g % 2 == 1:
                    dve.memset(acc[:, AC * (g - 1):AC * (g + 1)], 0.0)
            dve.memset(acc[:, AC * (NG - 1):NB * AW], 0.0)
            dve.wait_ge(consts, 1)

            def quad_rows(q, k):
                dve.tensor_copy(idx[:, k * TQ:(k + 1) * TQ], src_t[:, ds(q, 1), :]).then_inc(idx_ready, 1)

            def select(q, s, b):
                dve.tensor_scalar(rel[:, s, :], dst_t[:, ds(q, 1), :], block0[:, ds(b, 1)], None, ALU.subtract)
                dve.drain()
                for j in range(TQ):
                    last = dve.tensor_scalar(sel[:, s, j, :], lane[:, :], rel[:, s, j:j + 1], None, ALU.is_equal)
                last.then_inc(sel_ready, 1)

            def add(s, b):
                to = acc[:, ds(b * AW, AW)]
                dve.tensor_tensor(to, to, ps_q[s][:, 0:AW], ALU.add).then_inc(acc_done, 1)

            n = dve.alloc_register("visits")
            b = dve.alloc_register("visit_block")
            pending = dve.alloc_register("pending_block")
            regs = [dve.alloc_register(f"quad_blocks{i}") for i in range(2 * QS)]
            dve.reg_mov(n, 0)
            dve.reg_mov(pending, 0)
            for q in range(3):
                quad_rows(q, q)
            dve.drain()
            blk = dve.alloc_register("node_block")
            last, end, t_reg = (dve.alloc_register(m) for m in ("last_node_slot", "chunk_end", "slot"))

            def select_quad(t, k):
                q = t * QS + k
                dve.reg_mov(b, regs[2 * k])
                with dve.While(lambda: dve.snap(b) < dve.snap(regs[2 * k + 1])):
                    dve.wait_ge(visit_done, dve.snap(n) + 2)
                    select(q, (k + 1) % 2, dve.snap(b, min_val=0, max_val=NB - 1))
                    add((k + 1) % 2, dve.snap(pending, min_val=0, max_val=NB - 1))
                    dve.reg_mov(pending, b)
                    dve.reg_add(n, n, 1)
                    dve.reg_add(b, b, 1)
                dve.wait_ge(visit_done, dve.snap(n) + 1)
                select(q, k % 2, dve.snap(b, min_val=0, max_val=NB - 1))

            def add_last(t, k):
                dve.wait_ge(visit_done, dve.snap(n) + 2)
                add((k + 1) % 2, dve.snap(pending, min_val=0, max_val=NB - 1))
                dve.reg_mov(pending, b)
                dve.reg_add(n, n, 1)
                quad_rows(t * QS + k + 3, (k + 3) % QS)

            def block_of(t, known):
                if known is None:
                    dve.load([blk], ntab[0:1, ds(t, 1)])
                    return dve.snap(blk, min_val=0, max_val=NB - 2)
                return known

            def prepare_node(t, known=None):
                c = block_of(t, known)
                one = ds(c, 1)
                dve.wait_ge(xb_in, 16 * (t + 1))
                dve.tensor_scalar(cat[:, 0:D], xb[:, :], mean1[:, one], rstd1[:, one], ALU.subtract, ALU.mult)
                dve.tensor_scalar(sm[:, 20:21], acc[:, ds(c * AW + D, 1)], 1.0, None, ALU.max)
                dve.tensor_copy(sm[:, 26:27], node_id[:, one])
                dve.drain()
                dve.reciprocal(sm[:, 21:22], sm[:, 20:21])
                dve.drain()
                dve.tensor_scalar(cat[:, D:2 * D], acc[:, ds(c * AW, D)], sm[:, 21:22], None,
                                  ALU.mult).then_inc(cat_ready, 1)

            def finish_row(t):
                dve.wait_ge(count_ps, t + 1)
                dve.tensor_tensor(g8[:, 6, :], ps_h[:, 0:EX], seen[:, :], ALU.add)
                dve.tensor_scalar(sm[:, 24:25], sm[:, 19:20], float(-SLOTS), float((EX + RV) * SLOTS - 1),
                                  ALU.mult, ALU.add)
                dve.drain()
                dve.tensor_tensor(g8[:, 6, :], g8[:, 6, :], hot[:, :], ALU.mult)
                dve.tensor_tensor(seen[:, :], ps_h[:, EX:2 * EX], seen[:, :], ALU.add)
                dve.drain()
                dve.tensor_reduce(sm[:, 22:23], g8[:, 6, :], AX, ALU.max)
                dve.drain()
                dve.tensor_scalar(sm[:, 23:24], sm[:, 22:23], float(CAP), float(EX * SLOTS), ALU.is_gt, ALU.mult)
                dve.tensor_tensor(sm[:, 24:25], sm[:, 22:23], sm[:, 24:25], ALU.add)
                dve.drain()
                dve.tensor_tensor(slot[:, :], sm[:, 23:24], sm[:, 24:25], ALU.add).then_inc(row_ready, 1)

            def new_row(t):
                dve.wait_ge(zln_ready, t + 1)
                newton(sm[:, 4:5], sm[:, 0:1], sm[:, 2:3], sm[:, 3:4])
                dve.drain()
                dve.wait_ge(x1_out, 16 * (t + 1))
                dve.wait_ge(disp_out, 16 * (t + 1))
                dve.scalar_tensor_tensor(out=row[:, 0:D], in0=ps_b[:, 0:D], scalar=sm[:, 4:5], in1=xb[:, :],
                                         op0=ALU.mult, op1=ALU.add)
                dve.drain().then_inc(xb_free, 1)
                dve.tensor_tensor(row[:, 0:D], row[:, 0:D], gb_sb[:, :], ALU.add).then_inc(x1_ready, 1)
                dve.drain()
                dve.bn_stats(bn[:, :], row[:, 0:D])
                dve.drain()
                dve.bn_aggr(sm[:, 8:10], bn[:, :])
                dve.drain()
                dve.tensor_scalar(sm[:, 10:11], sm[:, 9:10], EPS, None, ALU.add).then_inc(var2_ready, 1)
                dve.tensor_copy(row[:, C_MEAN:C_MEAN + 1], sm[:, 8:9])
                dve.tensor_copy(row[:, C_NODE:C_NODE + 1], sm[:, 26:27])

            def normalise_row(t):
                dve.wait_ge(ln2_ready, t + 1)
                newton(row[:, C_RSTD:C_RSTD + 1], sm[:, 10:11], sm[:, 12:13], sm[:, 13:14])
                dve.drain()
                dve.tensor_scalar(cat[:, D:2 * D], row[:, 0:D], row[:, C_MEAN:C_MEAN + 1],
                                  row[:, C_RSTD:C_RSTD + 1], ALU.subtract, ALU.mult).then_inc(xl_ready, 1)

            def route(t):
                dve.wait_ge(logit_ps, t + 1)
                dve.tensor_tensor(g8[:, 0, :], ps_a[:, 3, 0:EX], gateb_sb[:, :], ALU.add)
                dve.drain()
                dve.tensor_reduce(sm[:, 16:17], g8[:, 0, :], AX, ALU.max, negate=True).then_inc(logit_ready, 1)
                dve.wait_ge(exp_ready, t + 1)
                dve.reciprocal(sm[:, 18:19], sm[:, 17:18])
                dve.drain()
                dve.tensor_scalar(g8[:, 2, :], g8[:, 1, :], sm[:, 18:19], None, ALU.mult)
                dve.drain()
                dve.tensor_reduce(row[:, C_GATE:C_GATE + 1], g8[:, 2, :], AX, ALU.max)
                dve.drain()
                dve.scalar_tensor_tensor(out=g8[:, 3, :], in0=g8[:, 2, :], scalar=row[:, C_GATE:C_GATE + 1],
                                         in1=rev9[:, :], op0=ALU.is_equal, op1=ALU.mult)
                dve.drain()
                dve.tensor_reduce(sm[:, 25:26], g8[:, 3, :], AX, ALU.max)
                dve.drain()
                dve.tensor_scalar(sm[:, 19:20], sm[:, 25:26], valid[:, ds(t, 1)], None, ALU.mult)
                dve.drain()
                dve.tensor_scalar(hot[:, :], rev9[:, :], sm[:, 19:20], None, ALU.is_equal).then_inc(hot_ready, 1)

            def choose(t, whole=True):
                lim, least = (float((CAP // P) * P), float(P)) if whole else (float(CAP), 1.0)
                have, cand, hit, take = (g8[0:1, r, :] for r in (4, 5, 4, 7))
                dve.scalar_tensor_tensor(out=have, in0=seen[0:1, :], scalar=lim, in1=taken[:, :],
                                         op0=ALU.min, op1=ALU.subtract)
                dve.drain()
                dve.scalar_tensor_tensor(out=cand, in0=have, scalar=least, in1=rev[0:1, :],
                                         op0=ALU.is_ge, op1=ALU.mult)
                dve.drain()
                dve.tensor_reduce(sm[0:1, 27:28], cand, AX, ALU.max)
                dve.drain()
                dve.tensor_scalar(hit, rev[0:1, :], sm[0:1, 27:28], None, ALU.is_equal)
                dve.tensor_scalar(sm[0:1, 28:29], sm[0:1, 27:28], 1.0, -1.0, ALU.max, ALU.mult)
                dve.drain()
                dve.tensor_tensor(take, hit, taken[:, :], ALU.mult)
                dve.tensor_scalar(ctab[0:1, ds(t + 2, 1), 1], sm[0:1, 28:29], float(EX), None, ALU.add)
                dve.drain()
                dve.tensor_reduce(sm[0:1, 29:30], take, AX, ALU.max)
                dve.scalar_tensor_tensor(out=taken[:, :], in0=hit, scalar=float(P), in1=taken[:, :],
                                         op0=ALU.mult, op1=ALU.add)
                dve.drain()
                dve.scalar_tensor_tensor(out=sm[0:1, 30:31], in0=sm[0:1, 27:28], scalar=float(-SLOTS),
                                         in1=sm[0:1, 29:30], op0=ALU.mult, op1=ALU.add)
                dve.drain()
                dve.tensor_scalar(ctab[0:1, ds(t + 2, 1), 0], sm[0:1, 30:31], float(EX * SLOTS), None, ALU.add)
                dve.drain().then_inc(code_ready, 1)

            def prepare_chunk(t):
                dve.wait_ge(xs_in, 16 * chunks(t))
                dve.tensor_scalar(hid[:, 0:D], xs[:, 0:D], xs[:, C_MEAN:C_MEAN + 1],
                                  xs[:, C_RSTD:C_RSTD + 1], ALU.subtract, ALU.mult).then_inc(xc_ready, 1)

            def hidden(t):
                c = chunks(t)
                dve.wait_ge(hid_ps, 2 * c - 1)
                dve.wait_ge(res_out, 16 * c)
                dve.tensor_copy(hid[:, 0:512], ps_h[:, 0:512]).then_inc(hid_ready, 1)

            def result(t):
                c = chunks(t)
                dve.wait_ge(y_ready, c)
                dve.wait_ge(ys_in, 32 * c)
                y, keep, lim = hid[:, 3 * D:4 * D], hid[:, 2 * D:3 * D], res
                dve.tensor_tensor(y, ps_b[:, 0:D], b2_b[:, :], ALU.add)
                dve.drain()
                dve.tensor_scalar(y, y, ys[:, C_GATE:C_GATE + 1], None, ALU.mult)
                dve.drain()
                dve.tensor_scalar(lim, y, -1e4, 1e4, ALU.max, ALU.min)
                dve.tensor_tensor(keep, y, y, ALU.is_equal)
                dve.drain()
                dve.tensor_tensor(lim, lim, keep, ALU.mult)
                dve.drain()
                dve.tensor_scalar(keep.bitcast(I32), y, 0.0, 0.0, ALU.mult, ALU.is_equal)
                dve.drain()
                dve.copy_predicated(lim, keep.bitcast(I32), y)
                dve.tensor_copy(node_i[:, :], ys[:, C_NODE:C_NODE + 1])
                dve.drain()
                dve.tensor_tensor(lim, lim, ys[:, 0:D], ALU.add)
                dve.drain().then_inc(res_ready, 1)

            def trip(t, quads=True, node=True, chunk=True, known=None, next_node=True, next_known=None):
                if quads:
                    dve.load(regs, qtab[0:1, ds(t * QS, QS), :])
                    select_quad(t, 0)
                    add_last(t, 0)
                if node:
                    finish_row(t)
                if quads:
                    select_quad(t, 1)
                if node:
                    new_row(t)
                if chunk:
                    hidden(t)
                if node:
                    normalise_row(t)
                if quads:
                    add_last(t, 1)
                    select_quad(t, 2)
                    add_last(t, 2)
                    select_quad(t, 3)
                if node:
                    route(t)
                if chunk and next_node:
                    choose(t, whole=node)
                if node and next_node:
                    prepare_node(t + 1, next_known)
                if chunk:
                    dve.wait_ge(hidt_ps, 2 * chunks(t))
                    prepare_chunk(t + 1)
                    result(t)
                if quads:
                    dve.drain()
                    add_last(t, 3)

            dve.sem_inc(res_ready, 1)
            dve.sem_inc(code_ready, 1)
            dve.wait_ge(const_in, 16 * 4)
            prepare_node(0)
            with dve.Fori(0, C0) as t:
                trip(t, chunk=False)
            prepare_chunk(C0)
            with dve.Fori(C0, TRIPS) as t:
                trip(t)
            dve.drain()
            dve.wait_ge(visit_done, dve.snap(n) + 2)
            add((NQ - 1) % 2, dve.snap(pending, min_val=0, max_val=NB - 1))
            dve.drain()
            dve.load([last], ends[0:1, 0:1])
            dve.reg_mov(t_reg, TRIPS)
            with dve.While(lambda: dve.snap(t_reg) + 1 < dve.snap(last)):
                trip(dve.snap(t_reg, min_val=TRIPS, max_val=TABW - 4), quads=False)
                dve.reg_add(t_reg, t_reg, 1)
            trip(dve.snap(t_reg, min_val=TRIPS, max_val=TABW - 4), quads=False, next_known=NB - 1)
            dve.reg_add(t_reg, t_reg, 1)
            trip(dve.snap(t_reg, min_val=TRIPS, max_val=TABW - 3), quads=False, known=NB - 1, next_node=False)
            dve.reg_add(t_reg, t_reg, 1)
            finish_row(dve.snap(t_reg))
            dve.drain()
            dve.tensor_scalar(g8[0:1, 4, :], seen[0:1, :], float(CAP), float(P - 1), ALU.min, ALU.add)
            dve.drain()
            dve.tensor_copy(left_i[:, :], g8[0:1, 4, :])
            dve.drain()
            dve.tensor_scalar(left_i[:, :], left_i[:, :], 7, None, ALU.logical_shift_right)
            dve.drain()
            dve.tensor_copy(g8[0:1, 5, :], left_i[:, :])
            dve.drain()
            dve.scalar_tensor_tensor(out=g8[0:1, 7, :], in0=taken[:, :], scalar=-1.0 / P, in1=g8[0:1, 5, :],
                                     op0=ALU.mult, op1=ALU.add)
            dve.drain()
            dve.tensor_reduce(sm[0:1, 27:28], g8[0:1, 7, :], AX, ALU.add)
            dve.drain()
            dve.scalar_tensor_tensor(out=sm[0:1, 28:29], in0=sm[0:1, 27:28], scalar=2.0, in1=last_f[:, :],
                                     op0=ALU.add, op1=ALU.add)
            dve.drain()
            dve.tensor_copy(ends[0:1, 1:2], sm[0:1, 28:29])
            dve.drain().then_inc(ends_ready, 1)
            choose(dve.snap(t_reg, min_val=TRIPS, max_val=NSLOTS - 3) - 1, whole=False)
            dve.load([end], ends[0:1, 1:2])
            with dve.While(lambda: dve.snap(t_reg) < dve.snap(end)):
                trip(dve.snap(t_reg, min_val=TRIPS, max_val=NSLOTS - 4), quads=False, node=False)
                dve.reg_add(t_reg, t_reg, 1)


_INS = ["x", "src", "dst", "L0_gnn_weight", "L0_gnn_bias", "L0_ffn_gate_w", "L0_ffn_gate_b",
        "L0_ffn_w1", "L0_ffn_b1", "L0_ffn_w2", "L0_ffn_b2"]


def kernel(**inputs):
    import concourse.bacc as _bacc
    from concourse.bass_utils import run_bass_kernel_spmd as _run

    nc = _bacc.Bacc("TRN2", target_bir_lowering=False, num_devices=1, dynamic_dma_scratch_size=2048)
    arrays, args = {}, []
    for name in _INS:
        a = np.ascontiguousarray(inputs[name])
        arrays[f"in_{name}"] = a
        args.append(nc.dram_tensor(f"in_{name}", a.shape, mybir.dt.from_np(a.dtype), kind="ExternalInput").ap())
    args.append(nc.dram_tensor("out_0", (N, D), FP32, kind="ExternalOutput").ap())
    gnn_moe_layer(nc, *args)
    r = _run(nc, [arrays], core_ids=[0])
    return r.results[0]["out_0"]
```

```python
import numpy as np
import concourse.bass as bass
from concourse import mybir
from contextlib import ExitStack

FP32 = mybir.dt.float32
BF16 = mybir.dt.bfloat16
I32 = mybir.dt.int32
I16 = mybir.dt.int16
ALU = mybir.AluOpType
ACT = mybir.ActivationFunctionType
AX = mybir.AxisListType.X

P = 128
N = 6250
D = 256
E_EDGES = 100000
NB = -(-N // P)
LAST = N - (NB - 1) * P
TQ = 4
QE = TQ * P
QH = 98
NQ = 2 * QH
QS = 4
FULLQ = E_EDGES // QE
TAIL = E_EDGES - FULLQ * QE
PAD_DST = 16383
NPART = 3
XG = 7
NG = NB // XG
EX = 8
F = 1024
JF = F // P
KD = D // P
CAP = -(-5 * N // (4 * EX))
CH = -(-CAP // P)
SLOTS = CH * P
ROW = 260
C_OFF, C_RSTD, C_GATE, C_NODE = D, D + 1, D + 2, D + 3
EPS = 1e-5
AW = D + 1
TRIPS = NQ // QS
C0 = EX
TABW = 2 * TRIPS + 6
NSLOTS = 2 * TRIPS + EX * CH + 6
RV = EX + 1
DISP_ROWS = EX * SLOTS + P
FAR = 1 << 20


def gnn_moe_layer(nc, x, src, dst, gnn_w, gnn_b, gate_w, gate_b, w1, b1, w2, b2, out):
    ds = bass.ds
    parts_d = nc.dram_tensor("parts_d", (N, NPART * D), BF16, kind="Internal").ap()
    disp_d = nc.dram_tensor("disp_d", (DISP_ROWS, ROW), FP32, kind="Internal").ap()

    ctx = ExitStack()
    with ctx:
        def sb(name, shape, dt):
            return ctx.enter_context(nc.sbuf_tensor(name, shape, dt))

        def pb(name, shape):
            return ctx.enter_context(nc.psum_tensor(name, shape, FP32))

        def sem(name):
            return ctx.enter_context(nc.semaphore(name))

        w1_sb = sb("w1_sb", [P, KD, EX * F], FP32)
        w2_sb = sb("w2_sb", [P, JF, EX * D], FP32)
        acc = sb("acc", [P, NB * AW], FP32)
        ring = sb("ring", [P, 2 * TQ, NPART * D], BF16)
        dst_t = sb("dst_t", [P, NQ + 3, TQ], I16)
        src_t = sb("src_t", [P, NQ + 3, TQ], I16)
        idx = sb("idx", [P, QS * TQ], I32)
        sel = sb("sel", [P, 2, TQ, P], BF16)
        ident = sb("ident", [P, P], FP32)
        tri = sb("tri", [P, P], BF16)
        ones = sb("ones", [P, P], BF16)
        ones_bf = sb("ones_bf", [P, 1], BF16)
        lane = sb("lane", [P, P], BF16)
        block0 = sb("block0", [P, NB], FP32)
        node_id = sb("node_id", [P, NB], FP32)
        rev = sb("rev", [P, EX], FP32)
        rev9 = sb("rev9", [P, EX], FP32)
        off1 = sb("off1", [P, NB], FP32)
        rstd1 = sb("rstd1", [P, NB], FP32)
        gw_sb = sb("gw_sb", [P, 2 * KD, D], FP32)
        gb_sb = sb("gb_sb", [P, D], FP32)
        gatew_sb = sb("gatew_sb", [P, KD, EX], FP32)
        gateb_sb = sb("gateb_sb", [P, EX], FP32)
        b1_t = sb("b1_t", [P, EX * JF], FP32)
        qtab = sb("qtab", [1, NQ + QS, 2], I16)
        ntab = sb("ntab", [1, TABW], I16)
        valid = sb("valid", [P, TABW], FP32)
        ctab = sb("ctab", [1, NSLOTS, 2], I16)
        ends = sb("ends", [1, 2], I16)
        last_f = sb("last_f", [1, 1], FP32)
        seen = sb("seen", [P, EX], FP32)
        taken = sb("taken", [1, EX], FP32)
        xb = sb("xb", [P, D], FP32)
        cat = sb("cat", [P, 2 * D], FP32)
        cat_t = sb("cat_t", [P, 2 * KD, P], FP32)
        row = sb("row", [P, ROW], FP32)
        slot = sb("slot", [P, 1], I32)
        left_i = sb("left_i", [1, EX], I32)
        sm = sb("sm", [P, 32], FP32)
        g8 = sb("g8", [P, 8, EX], FP32)
        hot = sb("hot", [P, EX], BF16)
        bn = sb("bn", [P, 6], FP32)
        xs = sb("xs", [P, ROW], FP32)
        ys = sb("ys", [P, ROW], FP32)
        b2_b = sb("b2_b", [P, D], FP32)
        hid = sb("hid", [P, F], FP32)
        hid_t = sb("hid_t", [P, JF, P], FP32)
        xc_t = hid_t[:, 0:KD, :]
        node_i = sb("node_i", [P, 1], I32)

        w1_flat = w1_sb[:, :, :].rearrange("p k f -> p (k f)")
        w2_flat = w2_sb[:, :, :].rearrange("p j f -> p (j f)")

        def carve(flat, at, n):
            return flat[:, at:at + n]

        XW = XG * D
        xin = [carve(w1_flat, s * XW, XW) for s in (0, 1, 6)]
        xn = [carve(w1_flat, (2 + s) * XW, XW) for s in range(2)]
        r1 = [carve(w1_flat, (4 + s) * XW, XW) for s in range(2)]
        parts = [carve(w2_flat, s * NPART * XW // 2, NPART * XW // 2).bitcast(BF16) for s in range(2)]
        at = NPART * XW
        dst_i = carve(w2_flat, at, 2 * QE).bitcast(I32)
        src_i = carve(w2_flat, at + 2 * QE, 2 * QE).bitcast(I32)
        dst_f = carve(w2_flat, at + 4 * QE, 2 * QE)
        src_f = carve(w2_flat, at + 6 * QE, 2 * QE)
        dst_m = carve(w2_flat, at + 8 * QE, 2 * QE)
        b1_r = w1_flat[0:EX * JF, 7 * XW:7 * XW + P]
        qmm = carve(w2_flat, at + 10 * QE, 4)
        qmi = carve(w2_flat, at + 10 * QE + 8, 4).bitcast(I32)
        qmf = carve(w2_flat, at + 10 * QE + 16, 4)
        bn1 = carve(w1_flat, 7 * XW + P, XG * 6)
        mv1 = carve(w1_flat, 7 * XW + P + 64, XG * 4)
        nt1 = carve(w1_flat, 7 * XW + P + 128, XG * 4)
        tabs = [carve(w2_flat, at + 10 * QE + 32 + i * 2 * TABW, 2 * TABW)[0:1, :] for i in range(4)]
        one_row = carve(w2_flat, at + 10 * QE + 32 + 8 * TABW, P)[0:1, :]

        ps_q = [pb(f"ps_q{i}", [P, 512]) for i in range(2)]
        ps_a = pb("ps_a", [P, 4, P])
        ps_b = pb("ps_b", [P, 512])
        ps_h = pb("ps_h", [P, F])
        ps_t = pb("ps_t", [P, JF, P])

        stage_clear = sem("stage_clear")
        stage_in = sem("stage_in")
        const_in = sem("const_in")
        b1_in = sem("b1_in")
        consts = sem("consts")
        pool_step = sem("pool_step")
        pool_turn = sem("pool_turn")
        sp_turn = sem("sp_turn")
        xin_in = [sem(f"xin_in{s}") for s in range(3)]
        xin_used = sem("xin_used")
        var1_ready = sem("var1_ready")
        ln1_ready = sem("ln1_ready")
        xn_ready = sem("xn_ready")
        r1_ready = sem("r1_ready")
        hi_copied = sem("hi_copied")
        low_done = sem("low_done")
        parts_out = [sem(f"parts_out{s}") for s in range(2)]
        stage_f = sem("stage_f")
        edges_t = sem("edges_t")
        edges_copied = sem("edges_copied")
        qblocks = sem("qblocks")
        qrow = sem("qrow")
        qtab_ready = sem("qtab_ready")
        weights_in = sem("weights_in")
        idx_ready = sem("idx_ready")
        gathered = [sem(f"gathered{s}") for s in range(4)]
        ring_free = sem("ring_free")
        sel_ready = sem("sel_ready")
        visit_done = sem("visit_done")
        acc_done = sem("acc_done")
        vrow = sem("vrow")
        valid_ps = sem("valid_ps")
        valid_ready = sem("valid_ready")
        xb_in = sem("xb_in")
        xb_free = sem("xb_free")
        cat_ready = sem("cat_ready")
        cat_ps = sem("cat_ps")
        catt_ready = sem("catt_ready")
        z_ready = sem("z_ready")
        norm_ready = sem("norm_ready")
        x1_ready = sem("x1_ready")
        var2_ready = sem("var2_ready")
        stat2_ready = sem("stat2_ready")
        deg_ready = sem("deg_ready")
        ln2_ready = sem("ln2_ready")
        xl_ready = sem("xl_ready")
        xl_ps = sem("xl_ps")
        xlt_ready = sem("xlt_ready")
        logit_ps = sem("logit_ps")
        logit_ready = sem("logit_ready")
        exp_ready = sem("exp_ready")
        hot_ready = sem("hot_ready")
        count_ps = sem("count_ps")
        row_ready = sem("row_ready")
        x1_out = sem("x1_out")
        disp_out = sem("disp_out")
        code_ready = sem("code_ready")
        ends_ready = sem("ends_ready")
        xs_in = sem("xs_in")
        ys_in = sem("ys_in")
        xc_ready = sem("xc_ready")
        xc_ps = sem("xc_ps")
        xct_ready = sem("xct_ready")
        hid_ps = sem("hid_ps")
        hid_ready = sem("hid_ready")
        hidt_ps = sem("hidt_ps")
        hidt_ready = sem("hidt_ready")
        y_ready = sem("y_ready")
        y_read = sem("y_read")
        res_ready = sem("res_ready")
        res_out = sem("res_out")

        block = ctx.enter_context(nc.Block())

        def chunks(t):
            return t - (C0 - 1)

        @block.sync
        def _(sp):
            def load_x(g):
                blocks = XG if g < NG - 1 else XG - 1
                sp.dma_start(xin[g % 3][:, 0:blocks * D].rearrange("p (b d) -> p b d", d=D),
                             x[ds(g * (XG * P), blocks * P), :].rearrange("(b p) d -> p b d", p=P)
                             ).then_inc(xin_in[g % 3], 16)
                if g == NG - 1:
                    sp.dma_start(xin[g % 3][0:LAST, (XG - 1) * D:XG * D], x[(NB - 1) * P:N, :]
                                 ).then_inc(xin_in[g % 3], 16)

            def store_parts(g, s, blocks):
                sp.dma_start(parts_d[ds(g * (XG * P), blocks * P), :].rearrange("(b p) d -> p b d", p=P),
                             parts[s][:, 0:blocks * NPART * D].rearrange("p (b d) -> p b d", d=NPART * D)
                             ).then_inc(parts_out[s], 16)

            load_x(0)
            load_x(1)
            sp.wait_ge(stage_clear, 1)
            for dram, staged in ((dst, dst_i), (src, src_i)):
                sp.dma_start(staged[0:QH, 0:QE],
                             dram[0:QH * QE].rearrange("(p e) -> p e", e=QE)).then_inc(stage_in, 16)
                sp.dma_start(staged[0:FULLQ - QH, QE:2 * QE],
                             dram[QH * QE:FULLQ * QE].rearrange("(p e) -> p e", e=QE)).then_inc(stage_in, 16)
                sp.dma_start(staged[FULLQ - QH:FULLQ - QH + 1, QE:QE + TAIL],
                             dram[FULLQ * QE:E_EDGES].rearrange("(p e) -> p e", p=1)).then_inc(stage_in, 16)
            sp.dma_start(b1_r, b1.rearrange("e (j p) -> (e j) p", p=P)).then_inc(b1_in, 16)

            load_x(2)
            for g in range(NG):
                s = g % 2
                if g + 3 < NG:
                    sp.wait_ge(xin_used, g + 1)
                    load_x(g + 3)
                sp.wait_ge(low_done, g + 1)
                sp.wait_ge(hi_copied, g + 1)
                if g < NG - 1:
                    store_parts(g, s, XG)
                else:
                    store_parts(g, s, XG - 1)
                    sp.dma_start(parts_d[(NB - 1) * P:N, :],
                                 parts[s][0:LAST, (XG - 1) * NPART * D:XG * NPART * D]).then_inc(parts_out[s], 16)
                if g == 0:
                    sp.wait_ge(consts, 1)
                    sp.dma_start(disp_d.rearrange("(t p) c -> p t c", p=P),
                                 row[:, :].rearrange("p (a c) -> p a c", a=1).to_broadcast((P, DISP_ROWS // P, ROW))
                                 ).then_inc(x1_out, 16)
            sp.wait_ge(parts_out[0], 16 * (NG // 2 + 2))
            sp.wait_ge(parts_out[1], 16 * (NG // 2))
            sp.wait_ge(valid_ready, 1)
            sp.wait_ge(edges_copied, 5)
            sp.sem_inc(sp_turn, 1)

            def load_weights(e, half):
                if half == 0:
                    for k in range(KD):
                        sp.dma_start(w1_sb[:, k, ds(e * F, F)],
                                     w1[ds(e, 1), k * P:(k + 1) * P, :].rearrange("e p f -> p (e f)")
                                     ).then_inc(weights_in, 16)
                else:
                    for j in range(0, JF, 4):
                        sp.dma_start(w2_sb[:, j:j + 4, ds(e * D, D)],
                                     w2[ds(e, 1), j * P:(j + 4) * P, :].rearrange("e (j p) f -> p (e j) f", p=P)
                                     ).then_inc(weights_in, 16)

            blk, blk2 = sp.alloc_register("node_block"), sp.alloc_register("next_node_block")
            code = [sp.alloc_register(n) for n in ("chunk_row", "chunk_expert")]
            last, end, t_reg = (sp.alloc_register(n) for n in ("last_node_slot", "chunk_end", "slot"))

            def next_block(t, known):
                if known is None:
                    sp.load([blk2], ntab[0:1, ds(t, 1)])
                    return sp.snap(sp.snap(blk2, min_val=0, max_val=NB - 2) * P)
                return known * P

            def load_node(t, known=None, rows=P):
                b = next_block(t, known)
                if not isinstance(t, int):
                    sp.wait_ge(xb_free, t)
                sp.dma_start(xb[0:rows, :], x[ds(b, rows), :]).then_inc(xb_in, 16)

            def load_xs(t):
                sp.sem_inc(sp_turn, 1)
                sp.load(code, ctab[0:1, ds(t, 1), :])
                sp.dma_start(xs[:, :], disp_d[ds(sp.snap(code[0], min_val=0, max_val=EX * SLOTS), P), :]
                             ).then_inc(xs_in, 16)

            def load_ys(t):
                sp.load(code, ctab[0:1, ds(t, 1), :])
                first = sp.snap(code[0], min_val=0, max_val=EX * SLOTS)
                e = sp.snap(code[1], min_val=0, max_val=EX - 1)
                if not isinstance(t, int):
                    sp.wait_ge(res_out, 16 * chunks(t))
                sp.dma_start(ys[:, :], disp_d[ds(first, P), :]).then_inc(ys_in, 16)
                sp.dma_start(b2_b[:, :], b2[ds(e, 1), :].to_broadcast((P, D))).then_inc(ys_in, 16)

            def trip(t, node=True, chunk=True, known=None, rows=P, next_known=None, next_rows=P, next_node=True,
                     weights=False, prev=True):
                if weights:
                    load_weights(t, 0)
                if node:
                    if known is None:
                        sp.load([blk], ntab[0:1, ds(t, 1)])
                    b = sp.snap(sp.snap(blk, min_val=0, max_val=NB - 2) * P) if known is None else known * P
                    sp.wait_ge(x1_ready, t + 1)
                    sp.dma_start(out[ds(b, rows), :], row[0:rows, 0:D]).then_inc(x1_out, 16)
                    if next_node:
                        load_node(t + 1, next_known, next_rows)
                if weights:
                    load_weights(t, 1)
                if chunk:
                    sp.wait_ge(code_ready, chunks(t))
                    sp.wait_ge(xc_ready, chunks(t))
                    if prev:
                        sp.sem_inc(sp_turn, 1)
                        sp.wait_ge(disp_out, 16 * t)
                        sp.wait_ge(x1_out, 16 * t)
                    load_xs(t + 1)
                    load_ys(t)

            sp.wait_ge(qtab_ready, 2)
            sp.wait_ge(x1_out, 16)
            sp.sem_inc(sp_turn, 1)
            load_node(0)
            with sp.Fori(0, C0) as t:
                trip(t, chunk=False, weights=True)
            load_xs(C0)
            load_ys(C0 - 1)
            with sp.Fori(C0, TRIPS) as t:
                trip(t)
            sp.load([last], ends[0:1, 0:1])
            sp.reg_mov(t_reg, TRIPS)
            with sp.While(lambda: sp.snap(t_reg) + 1 < sp.snap(last)):
                trip(sp.snap(t_reg, min_val=TRIPS, max_val=TABW - 4))
                sp.reg_add(t_reg, t_reg, 1)
            trip(sp.snap(t_reg, min_val=TRIPS, max_val=TABW - 4), next_known=NB - 1, next_rows=LAST)
            sp.reg_add(t_reg, t_reg, 1)
            trip(sp.snap(t_reg, min_val=TRIPS, max_val=TABW - 3), known=NB - 1, rows=LAST, next_node=False)
            sp.reg_add(t_reg, t_reg, 1)
            trip(sp.snap(t_reg, min_val=TRIPS, max_val=TABW - 2), node=False)
            sp.reg_add(t_reg, t_reg, 1)
            sp.wait_ge(disp_out, 16 * sp.snap(t_reg))
            sp.wait_ge(x1_out, 16 * sp.snap(t_reg))
            sp.wait_ge(ends_ready, 1)
            sp.sem_inc(sp_turn, 1)
            sp.load([end], ends[0:1, 1:2])
            with sp.While(lambda: sp.snap(t_reg) < sp.snap(end)):
                trip(sp.snap(t_reg, min_val=TRIPS, max_val=NSLOTS - 3), node=False, prev=False)
                sp.reg_add(t_reg, t_reg, 1)
            sp.wait_ge(ys_in, 32 * (sp.snap(t_reg) - C0 + 1))
            sp.wait_ge(xs_in, 16 * (sp.snap(t_reg) - C0 + 1))
            sp.sem_inc(sp_turn, 1)

        @block.gpsimd
        def _(pool):
            pool.memset(dst_i[:, :], PAD_DST)
            pool.memset(src_i[:, :], 0).then_inc(stage_clear, 1)
            pool.memset(ident[:, :], 0.0)
            pool.memset(tri[:, :], 1.0)
            pool.memset(ones[:, :], 1.0)
            pool.memset(seen[:, :], 0.0)
            pool.memset(taken[:, :], 0.0)
            pool.memset(one_row[:, :], 1.0)
            pool.memset(ctab[:, :, 0:1], EX * SLOTS)
            pool.memset(ctab[:, :, 1:2], EX - 1)
            pool.memset(hot[:, :], 0.0)
            pool.memset(sm[:, :], 0.0)
            pool.memset(node_i[:, :], FAR)
            pool.memset(row[:, 0:C_NODE], 0.0)
            pool.memset(row[:, C_NODE:C_NODE + 1], float(FAR))
            pool.memset(xb[:, :], 0.0)
            pool.memset(ones_bf[:, :], 1.0).then_inc(pool_step, 1)
            pool.iota(lane[:, :], [[1, P]], base=0, channel_multiplier=0, allow_small_or_imprecise_dtypes=True)
            pool.iota(block0[:, :], [[P, NB]], base=0, channel_multiplier=0, allow_small_or_imprecise_dtypes=True)
            pool.iota(node_id[:, :], [[P, NB]], base=0, channel_multiplier=1, allow_small_or_imprecise_dtypes=True)
            pool.iota(rev[:, :], [[-1, EX]], base=EX, channel_multiplier=0, allow_small_or_imprecise_dtypes=True)
            pool.iota(rev9[:, :], [[-1, EX]], base=EX + RV, channel_multiplier=0,
                      allow_small_or_imprecise_dtypes=True)
            pool.iota(tabs[0][:, 0:2 * TABW], [[1, 2 * TABW]], base=0, channel_multiplier=0,
                      allow_small_or_imprecise_dtypes=True)
            pool.wait_ge(pool_step, 1)
            pool.affine_select(out=ident[:, :], in_=ident[:, :], compare_op=ALU.not_equal, fill=1.0,
                               base=0, pattern=[[-1, P]], channel_multiplier=1)
            pool.affine_select(out=tri[:, :], in_=tri[:, :], compare_op=ALU.is_ge, fill=0.0,
                               base=0, pattern=[[1, P]], channel_multiplier=-1).then_inc(consts, 1)
            for view, dram in ((gb_sb[:, :], gnn_b.rearrange("(a n) -> a n", a=1).to_broadcast((P, D))),
                               (gateb_sb[:, :], gate_b.rearrange("(a n) -> a n", a=1).to_broadcast((P, EX))),
                               (gw_sb[:, :, :], gnn_w.rearrange("(k p) n -> p k n", p=P)),
                               (gatew_sb[:, :, :], gate_w.rearrange("(k p) n -> p k n", p=P))):
                pool.dma_start(view, dram).then_inc(const_in, 16)
            AC = NB * AW // NG
            for g in range(NG):
                s = g % 2
                pool.memset(acc[:, g * AC:(g + 1) * AC], 0.0)
                pool.wait_ge(r1_ready, g + 1)
                if g >= 2:
                    pool.wait_ge(parts_out[s], 16 * (g // 2))
                pool.tensor_tensor(
                    out=parts[s][:, :].rearrange("p (b k d) -> p b k d", k=NPART, d=D)[:, :, 2, :],
                    in0=r1[s][:, :].rearrange("p (b d) -> p b d", d=D),
                    in1=r1[s][:, :].bitcast(BF16).rearrange("p (b d t) -> p b d t", d=D, t=2)[:, :, :, 1],
                    op=ALU.subtract).then_inc(low_done, 1)
            pool.wait_ge(parts_out[0], 16 * (NG // 2 + 2))
            pool.wait_ge(parts_out[1], 16 * (NG // 2))
            last, end, t_reg = (pool.alloc_register(n) for n in ("last_node_slot", "chunk_end", "slot"))

            def gather(t, k, half):
                free = pool.snap((t * QS + k) * TQ + 2 * half + 2)
                turn = pool.snap(t * QS + (k + 1))
                pool.wait_ge(idx_ready, turn)
                pool.wait_ge(ring_free, free)
                pool.sem_inc(pool_turn, 1)
                for j in (2 * half, 2 * half + 1):
                    pool.indirect_dma_start(
                        ring[:, (k % 2) * TQ + j, :], None, parts_d[:, :],
                        bass.IndirectOffsetOnAxis(ap=idx[:, k * TQ + j:k * TQ + j + 1], axis=0)
                    ).then_inc(gathered[(2 * k + half) % 4], 16)

            def dispatch(t, rows=P):
                pool.wait_ge(x1_out, 16)
                pool.wait_ge(row_ready, t + 1)
                pool.sem_inc(pool_turn, 1)
                pool.indirect_dma_start(
                    disp_d[:, :], bass.IndirectOffsetOnAxis(ap=slot[0:rows, 0:1], axis=0), row[0:rows, :], None,
                    bounds_check=EX * SLOTS - 1, oob_is_err=False).then_inc(disp_out, 16)

            def results(t):
                pool.wait_ge(res_ready, chunks(t))
                pool.sem_inc(pool_turn, 1)
                pool.indirect_dma_start(
                    out[:, :], bass.IndirectOffsetOnAxis(ap=node_i[:, 0:1], axis=0), ys[:, 0:D], None,
                    bounds_check=N - 1, oob_is_err=False).then_inc(res_out, 16)

            def trip(t, quads=True, prev=True, chunk=True, rows=P):
                for k in range(QS):
                    for half in range(2):
                        if quads:
                            gather(t, k, half)
                if prev:
                    dispatch(t, rows)
                if chunk:
                    results(t)

            with pool.Fori(0, C0) as t:
                trip(t, chunk=False)
            with pool.Fori(C0, TRIPS) as t:
                trip(t)
            pool.load([last], ends[0:1, 0:1])
            pool.reg_mov(t_reg, TRIPS)
            with pool.While(lambda: pool.snap(t_reg) < pool.snap(last) + 1):
                trip(pool.snap(t_reg), quads=False)
                pool.reg_add(t_reg, t_reg, 1)
            trip(pool.snap(t_reg), quads=False, rows=LAST)
            pool.reg_add(t_reg, t_reg, 1)
            pool.wait_ge(ends_ready, 1)
            pool.sem_inc(pool_turn, 1)
            pool.load([end], ends[0:1, 1:2])
            with pool.While(lambda: pool.snap(t_reg) < pool.snap(end)):
                trip(pool.snap(t_reg), quads=False, prev=False)
                pool.reg_add(t_reg, t_reg, 1)
            results(pool.snap(t_reg))
            pool.wait_ge(res_out, 16 * (pool.snap(t_reg) - C0 + 1))

        @block.scalar
        def _(act):
            def rsqrt_start(to, of, tmp):
                act.activation(tmp, of, ACT.Ln)
                act.drain()
                return act.activation(to, tmp, ACT.Exp, scale=-0.5)

            act.preload_act_table_set("natural_log_exp_and_others")
            act.wait_ge(consts, 1)
            for g in range(NG):
                s = g % 2
                act.wait_ge(var1_ready, g + 1)
                o = (g % 2) * 2 * XG
                rsqrt_start(nt1[:, o + XG:o + 2 * XG], mv1[:, o + 1:o + 2 * XG:2], nt1[:, o:o + XG]
                            ).then_inc(ln1_ready, 1)
                view = parts[s][:, :].rearrange("p (b k d) -> p b k d", k=NPART, d=D)
                act.wait_ge(xn_ready, g + 1)
                if g >= 2:
                    act.wait_ge(parts_out[s], 16 * (g // 2))
                act.activation(view[:, :, 0, :],
                               xn[s][:, :].bitcast(BF16).rearrange("p (b d t) -> p b d t", d=D, t=2)[:, :, :, 1],
                               ACT.Copy)
                act.wait_ge(r1_ready, g + 1)
                act.activation(view[:, :, 1, :],
                               r1[s][:, :].bitcast(BF16).rearrange("p (b d t) -> p b d t", d=D, t=2)[:, :, :, 1],
                               ACT.Copy).then_inc(hi_copied, 1)
                if g == 1:
                    for m, to in enumerate((dst_t, src_t)):
                        for h in range(2):
                            act.wait_ge(edges_t, 2 * m + h + 1)
                            act.activation(to[:, h * QH:(h + 1) * QH, :].rearrange("p q j -> p j q"),
                                           ps_a[:, :, 0:QH], ACT.Copy).then_inc(edges_copied, 1)
                    act.wait_ge(edges_t, 5)
                    act.activation(b1_t[:, :], ps_a[:, 0, 0:EX * JF], ACT.Copy).then_inc(edges_copied, 1)

            blk = act.alloc_register("node_block")
            code = [act.alloc_register(n) for n in ("chunk_row", "chunk_expert")]
            last, end, t_reg = (act.alloc_register(n) for n in ("last_node_slot", "chunk_end", "slot"))

            def prepare_node(t, known=None):
                act.wait_ge(xb_in, 16 * (t + 1))
                act.wait_ge(deg_ready, t + 1)
                act.activation(cat[:, 0:D], xb[:, :], ACT.Identity, scale=rstd1[:, ds(known, 1)],
                               bias=off1[:, ds(known, 1)])
                act.activation(cat[:, D:2 * D], acc[:, ds(known * AW, D)], ACT.Identity, scale=sm[:, 21:22]
                               ).then_inc(cat_ready, 1)

            def trip(t, node=True, prev=True, chunk=True, known=None):
                c = chunks(t)
                if node and known is None:
                    act.load([blk], ntab[0:1, ds(t, 1)])
                    known = act.snap(blk, min_val=0, max_val=NB - 2)
                if prev:
                    act.wait_ge(xl_ps, t + 1)
                    act.activation(cat_t[:, 0:KD, :], ps_a[:, 0:KD, :], ACT.Copy).then_inc(xlt_ready, 1)
                if node:
                    prepare_node(t, known)
                if chunk:
                    act.wait_ge(xs_in, 16 * c)
                    act.activation(hid[:, 0:D], xs[:, 0:D], ACT.Identity, scale=xs[:, C_RSTD:C_RSTD + 1],
                                   bias=xs[:, C_OFF:C_OFF + 1]).then_inc(xc_ready, 1)
                    act.load(code, ctab[0:1, ds(t, 1), :])
                    e = act.snap(code[1], min_val=0, max_val=EX - 1)
                if node:
                    act.wait_ge(cat_ps, t + 1)
                    act.activation(cat_t[:, :, :], ps_a[:, :, :], ACT.Copy).then_inc(catt_ready, 1)
                if chunk:
                    act.wait_ge(xc_ps, c)
                    act.activation(xc_t, ps_t[:, 0:KD, :], ACT.Copy).then_inc(xct_ready, 1)
                if prev:
                    act.wait_ge(logit_ready, t + 1)
                    act.activation(g8[:, 1, :], g8[:, 0, :], ACT.Exp, bias=sm[:, 16:17],
                                   accum_out=sm[:, 17:18]).then_inc(exp_ready, 1)
                if node:
                    act.wait_ge(z_ready, t + 1)
                    act.activation(hid_t[:, KD:2 * KD, :], ps_a[:, 0:KD, :], ACT.Square,
                                   accum_out=sm[:, 0:1])
                    act.drain()
                    rsqrt_start(sm[:, 2:3], sm[:, 0:1], sm[:, 1:2]).then_inc(norm_ready, 1)
                if chunk:
                    for h in range(2):
                        act.wait_ge(hid_ps, 2 * c - 1 + h)
                        act.activation(hid[:, h * 512:(h + 1) * 512], ps_h[:, h * 512:(h + 1) * 512],
                                       ACT.Copy).then_inc(hid_ready, 1)
                if chunk:
                    for h in range(2):
                        act.wait_ge(hidt_ps, 2 * c - 1 + h)
                        for j in range(h * 4, h * 4 + 4):
                            done = act.activation(hid_t[:, j, :], ps_t[:, j, :], ACT.Relu,
                                                  bias=b1_t[:, ds(e * JF + j, 1)])
                        done.then_inc(hidt_ready, 1)
                if node:
                    act.wait_ge(var2_ready, t + 1)
                    rsqrt_start(sm[:, 12:13], sm[:, 10:11], sm[:, 11:12]).then_inc(ln2_ready, 1)
                if node:
                    act.wait_ge(stat2_ready, t + 1)
                    act.activation(cat[:, D:2 * D], row[:, 0:D], ACT.Identity, scale=row[:, C_RSTD:C_RSTD + 1],
                                   bias=row[:, C_OFF:C_OFF + 1]).then_inc(xl_ready, 1)

            with act.Fori(0, C0) as t:
                trip(t, chunk=False)
            with act.Fori(C0, TRIPS) as t:
                trip(t)
            act.load([last], ends[0:1, 0:1])
            act.reg_mov(t_reg, TRIPS)
            with act.While(lambda: act.snap(t_reg) < act.snap(last)):
                trip(act.snap(t_reg, min_val=0, max_val=TABW - 3))
                act.reg_add(t_reg, t_reg, 1)
            trip(act.snap(t_reg, min_val=0, max_val=TABW - 2), known=NB - 1)
            act.reg_add(t_reg, t_reg, 1)
            trip(act.snap(t_reg, min_val=0, max_val=TABW - 1), node=False)
            act.reg_add(t_reg, t_reg, 1)
            act.wait_ge(ends_ready, 1)
            act.load([end], ends[0:1, 1:2])
            with act.While(lambda: act.snap(t_reg) < act.snap(end)):
                trip(act.snap(t_reg, min_val=0, max_val=NSLOTS - 1), node=False, prev=False)
                act.reg_add(t_reg, t_reg, 1)

        @block.tensor
        def _(pe):
            pe.sem_inc(ring_free, 2 * TQ)
            pe.sem_inc(xl_ps, 1)
            pe.sem_inc(y_ready, 1)
            pe.sem_inc(visit_done, 2)
            pe.wait_ge(consts, 1)
            pe.wait_ge(stage_f, 1)
            for m, staged in enumerate((dst_f, src_f)):
                for h in range(2):
                    if m or h:
                        pe.wait_ge(edges_copied, 2 * m + h)
                    for j in range(TQ):
                        last = pe.transpose(ps_a[:, j, 0:QH], staged[0:QH, h * QE + j * P:h * QE + (j + 1) * P],
                                            ident[0:QH, 0:QH])
                    last.then_inc(edges_t, 1)
            pe.wait_ge(b1_in, 16)
            pe.wait_ge(edges_copied, 4)
            pe.transpose(ps_a[:, 0, 0:EX * JF], b1_r, ident[0:EX * JF, 0:EX * JF]).then_inc(edges_t, 1)
            pe.wait_ge(qblocks, 1)
            for m in range(4):
                last = pe.matmul(ps_b[0:1, m * QH:(m + 1) * QH], qmf[0:QH, m:m + 1], ident[0:QH, 0:QH],
                                 start=True, stop=True)
            last.then_inc(qrow, 1)

            pe.wait_ge(vrow, 1)
            pe.matmul(ps_b[:, 0:TABW], one_row[:, 0:P], tabs[3][:, 0:TABW], start=True, stop=True
                      ).then_inc(valid_ps, 1)

            n = pe.alloc_register("visits")
            b = pe.alloc_register("visit_block")
            pe.reg_mov(n, 0)
            regs = [pe.alloc_register(f"quad_blocks{i}") for i in range(2 * QS)]
            code = [pe.alloc_register(m) for m in ("chunk_row", "chunk_expert")]
            last, end, t_reg = (pe.alloc_register(m) for m in ("last_node_slot", "chunk_end", "slot"))
            pe.wait_ge(qtab_ready, 2)

            def visit(t, k, s, final, between=()):
                ps = ps_q[s]
                for j in range(TQ):
                    if j % 2 == 0:
                        pe.wait_ge(gathered[(2 * k + j // 2) % 4], 32 * (2 * t + k // 2 + 1))
                    for part in range(NPART):
                        mm = pe.matmul(ps[:, 0:D], sel[:, s, j, :],
                                       ring[:, (k % 2) * TQ + j, part * D:(part + 1) * D],
                                       start=(j == 0 and part == 0), stop=(j == TQ - 1 and part == NPART - 1),
                                       skip_group_check=True)
                    if final:
                        mm.then_inc(ring_free, 1)
                    mm = pe.matmul(ps[:, D:AW], sel[:, s, j, :], ones_bf[:, :], start=False,
                                   stop=(j == TQ - 1), skip_group_check=True)
                    if j == TQ - 1:
                        mm.then_inc(visit_done, 1)
                    if j < len(between):
                        between[j]()

            def quad(t, k, between):
                pe.reg_mov(b, regs[2 * k])
                with pe.While(lambda: pe.snap(b) < pe.snap(regs[2 * k + 1])):
                    pe.wait_ge(sel_ready, pe.snap(n) + 1)
                    pe.wait_ge(acc_done, pe.snap(n) + 2)
                    visit(t, k, (k + 1) % 2, False)
                    pe.reg_add(n, n, 1)
                    pe.reg_add(b, b, 1)
                pe.wait_ge(sel_ready, pe.snap(n) + 1)
                pe.wait_ge(acc_done, pe.snap(n) + 1)
                visit(t, k, k % 2, True, between)
                pe.reg_add(n, n, 1)

            def trip(t, quads=True, node=True, prev=True, chunk=True, rows=P):
                c = chunks(t)
                expert = []

                def load_expert():
                    pe.load(code, ctab[0:1, ds(t, 1), :])
                    expert.append(pe.snap(code[1], min_val=0, max_val=EX - 1))

                def load_quads():
                    pe.load(regs, qtab[0:1, ds(t * QS + QS, QS), :])

                def cat_transposes():
                    pe.wait_ge(cat_ready, t + 1)
                    for k in range(2 * KD):
                        last_ = pe.transpose(ps_a[:, k, :], cat[:, k * P:(k + 1) * P], ident[:, :])
                    last_.then_inc(cat_ps, 1)

                def xc_transposes():
                    pe.wait_ge(xc_ready, c)
                    for k in range(KD):
                        last_ = pe.transpose(ps_t[:, k, :], hid[:, k * P:(k + 1) * P], ident[:, :])
                    last_.then_inc(xc_ps, 1)

                def linear(h):
                    if h == 0:
                        pe.wait_ge(catt_ready, t + 1)
                    for k in (2 * h, 2 * h + 1):
                        last_ = pe.matmul(ps_a[:, 0:KD, :], cat_t[:, k, :], gw_sb[:, k, :],
                                          start=(k == 0), stop=(k == 2 * KD - 1))
                    if h == 1:
                        last_.then_inc(z_ready, 1)

                def up(h):
                    if h == 0:
                        pe.wait_ge(xct_ready, c)
                    for k in range(KD):
                        last_ = pe.matmul(ps_h[:, h * 512:(h + 1) * 512], xc_t[:, k, :],
                                          w1_sb[:, k, ds(expert[0] * F + h * 512, 512)],
                                          start=(k == 0), stop=(k == KD - 1))
                    last_.then_inc(hid_ps, 1)

                def hid_transposes(h):
                    pe.wait_ge(hid_ready, 2 * c - 1 + h)
                    for j in range(h * 4, h * 4 + 4):
                        last_ = pe.transpose(ps_t[:, j, :], hid[:, j * P:(j + 1) * P], ident[:, :])
                    last_.then_inc(hidt_ps, 1)

                def down(js):
                    for j in js:
                        if j == 0:
                            pe.wait_ge(y_read, c)
                            if prev:
                                pe.wait_ge(row_ready, t + 1)
                        if j % 4 == 0:
                            pe.wait_ge(hidt_ready, 2 * c - 1 + j // 4)
                        last_ = pe.matmul(ps_b[:, 0:D], hid_t[:, j, :], w2_sb[:, j, ds(expert[0] * D, D)],
                                          start=(j == 0), stop=(j == JF - 1))
                    if js[-1] == JF - 1:
                        last_.then_inc(y_ready, 1)

                def xl_transposes():
                    pe.wait_ge(xl_ready, t + 1)
                    for k in range(KD):
                        last_ = pe.transpose(ps_a[:, k, :], cat[:, D + k * P:D + (k + 1) * P], ident[:, :])
                    last_.then_inc(xl_ps, 1)

                def gate():
                    pe.wait_ge(xlt_ready, t + 1)
                    for k in range(KD):
                        last_ = pe.matmul(ps_b[:, D + 2 * EX:D + 3 * EX], cat_t[:, k, :], gatew_sb[:, k, :],
                                          start=(k == 0), stop=(k == KD - 1))
                    last_.then_inc(logit_ps, 1)

                def counts():
                    pe.wait_ge(hot_ready, t + 1)
                    if chunk:
                        pe.wait_ge(y_read, c)
                    pe.matmul(ps_b[:, D:D + EX], tri[0:rows, :], hot[0:rows, :], start=True, stop=True)
                    pe.matmul(ps_b[:, D + EX:D + 2 * EX], ones[0:rows, :], hot[0:rows, :],
                              start=True, stop=True).then_inc(count_ps, 1)

                def steps(*parts_):
                    def run():
                        for on, f, *args in parts_:
                            if on:
                                f(*args)
                    return run

                plan = [[steps((prev, gate), (chunk, load_expert)),
                         steps(),
                         steps((node, cat_transposes), (chunk, xc_transposes)),
                         steps()],
                        [steps((node, linear, 0)),
                         steps((node, linear, 1)),
                         steps((chunk, up, 0)),
                         steps()],
                        [steps((prev, counts), (chunk, up, 1)),
                         steps((chunk, hid_transposes, 0)),
                         steps((chunk, hid_transposes, 1)),
                         steps((chunk, down, (0, 1)))],
                        [steps((quads, load_quads), (chunk, down, (2, 3))),
                         steps((chunk, down, (4, 5))),
                         steps((chunk, down, (6, 7))),
                         steps((node, xl_transposes))]]
                for k in range(QS):
                    if quads:
                        quad(t, k, plan[k])
                    else:
                        for step in plan[k]:
                            step()

            pe.load(regs, qtab[0:1, 0:QS, :])
            with pe.Fori(0, C0) as t:
                trip(t, chunk=False)
            pe.wait_ge(weights_in, 16 * EX * (KD + JF // 4))
            with pe.Fori(C0, TRIPS) as t:
                trip(t)
            pe.load([last], ends[0:1, 0:1])
            pe.reg_mov(t_reg, TRIPS)
            with pe.While(lambda: pe.snap(t_reg) < pe.snap(last) + 1):
                trip(pe.snap(t_reg, min_val=0, max_val=TABW - 2), quads=False)
                pe.reg_add(t_reg, t_reg, 1)
            trip(pe.snap(t_reg, min_val=0, max_val=TABW - 1), quads=False, node=False, rows=LAST)
            pe.reg_add(t_reg, t_reg, 1)
            pe.wait_ge(ends_ready, 1)
            pe.load([end], ends[0:1, 1:2])
            with pe.While(lambda: pe.snap(t_reg) < pe.snap(end)):
                trip(pe.snap(t_reg, min_val=0, max_val=NSLOTS - 1), quads=False, node=False, prev=False)
                pe.reg_add(t_reg, t_reg, 1)

        @block.vector
        def _(dve):
            def newton(to, v, r, tmp):
                dve.tensor_tensor(tmp, v, r, ALU.mult)
                dve.drain()
                dve.tensor_tensor(tmp, tmp, r, ALU.mult)
                dve.drain()
                dve.tensor_scalar(tmp, tmp, -0.5, 1.5, ALU.mult, ALU.add)
                dve.drain()
                return dve.tensor_tensor(to, tmp, r, ALU.mult)

            def half_newton(v, r, to):
                dve.scalar_tensor_tensor(out=to, in0=v, scalar=r, in1=r, op0=ALU.mult, op1=ALU.mult)
                dve.drain()
                return dve.tensor_scalar(to, to, -0.5, 1.5, ALU.mult, ALU.add)

            dve.sem_inc(acc_done, 1)

            def edge_lists():
                dve.memset(src_t[:, NQ:NQ + 3, :], 0)
                dve.memset(dst_t[:, NQ:NQ + 3, :], PAD_DST)
                dve.memset(ps_q[1][:, 0:AW], 0.0)
                dve.wait_ge(stage_in, 16 * 6)
                dve.tensor_copy(dst_f[0:QH, :], dst_i[0:QH, :])
                dve.tensor_copy(src_f[0:QH, :], src_i[0:QH, :]).then_inc(stage_f, 1)
                dve.drain()
                dve.scalar_tensor_tensor(out=dst_m[0:QH, :], in0=dst_f[0:QH, :], scalar=float(N), in1=dst_f[0:QH, :],
                                         op0=ALU.is_lt, op1=ALU.mult)
                dve.drain()
                dve.tensor_reduce(qmm[0:QH, 0:2], dst_f[0:QH, :].rearrange("p (h e) -> p h e", h=2), AX, ALU.min)
                dve.tensor_reduce(qmm[0:QH, 2:4], dst_m[0:QH, :].rearrange("p (h e) -> p h e", h=2), AX, ALU.max)
                dve.drain()
                dve.tensor_copy(qmi[0:QH, :], qmm[0:QH, :])
                dve.drain()
                dve.tensor_scalar(qmi[0:QH, :], qmi[0:QH, :], 7, None, ALU.logical_shift_right)
                dve.drain()
                dve.tensor_copy(qmf[0:QH, :], qmi[0:QH, :]).then_inc(qblocks, 1)
                dve.wait_ge(qrow, 1)
                dve.memset(qtab[0:1, NQ:NQ + QS, :], 0)
                dve.tensor_copy(qtab[0:1, 0:NQ, :].rearrange("o q m -> o m q"),
                                ps_b[0:1, 0:4 * QH].rearrange("o (m q) -> o m q", m=2)).then_inc(qtab_ready, 1)

            def slot_tables():
                count, ta, tb, tc = tabs
                dve.memset(ta[:, :], float(NB))
                dve.drain()
                dve.tensor_reduce(ta[:, 0:TRIPS], ps_b[0:1, 0:NQ].rearrange("o (u k) -> o u k", k=QS), AX, ALU.min)
                dve.drain()
                cur, other = ta, tb
                step = 1
                while step < TRIPS:
                    dve.tensor_tensor(other[:, 0:TABW - step], cur[:, 0:TABW - step], cur[:, step:TABW],
                                      ALU.min)
                    dve.tensor_copy(other[:, TABW - step:TABW], cur[:, TABW - step:TABW])
                    dve.drain()
                    cur, other = other, cur
                    step *= 2
                dve.memset(tc[:, 0:2], 0.0)
                dve.tensor_copy(tc[:, 2:TABW], cur[:, 1:TABW - 1])
                dve.drain()
                dve.tensor_tensor(ta[:, 0:TABW], tc[:, 0:TABW], count[:, 0:TABW], ALU.subtract)
                dve.drain()
                cur, other = ta, tb
                step = 1
                while step < TABW:
                    dve.tensor_tensor(other[:, step:TABW], cur[:, step:TABW], cur[:, 0:TABW - step], ALU.min)
                    dve.tensor_copy(other[:, 0:step], cur[:, 0:step])
                    dve.drain()
                    cur, other = other, cur
                    step *= 2
                dve.memset(other[:, 0:1], 0.0)
                dve.tensor_tensor(other[:, 1:TABW], cur[:, 0:TABW - 1], count[:, 0:TABW - 1], ALU.add)
                dve.drain()
                dve.tensor_copy(ntab[:, :], other[:, 0:TABW])
                dve.tensor_scalar(last_f[:, :], other[:, TRIPS + 1:TRIPS + 2], -1.0, float(TRIPS + NB), ALU.mult, ALU.add)
                dve.tensor_tensor(tc[:, 0:TABW - 1], other[:, 1:TABW], other[:, 0:TABW - 1], ALU.subtract)
                dve.memset(tc[:, TABW - 1:TABW], 0.0)
                dve.drain().then_inc(vrow, 1)
                dve.tensor_copy(ends[:, 0:1], last_f[:, :]).then_inc(qtab_ready, 1)
                dve.wait_ge(valid_ps, 1)
                dve.memset(valid[:, 0:1], 0.0)
                dve.tensor_copy(valid[:, 1:TABW], ps_b[:, 0:TABW - 1])
                dve.drain().then_inc(valid_ready, 1)
                dve.memset(ps_b[:, 0:D], 0.0)
                dve.memset(ps_a[:, :, :], 0.0)

            def stats(g):
                s = g % 2
                dve.wait_ge(xin_in[g % 3], 16 * (g // 3 + (1 if g < NG - 1 else 2)))
                x_g = xin[g % 3][:, :].rearrange("p (b d) -> p b d", d=D)
                o = s * 2 * XG
                for b in range(XG):
                    dve.bn_stats(bn1[:, b * 6:(b + 1) * 6], x_g[:, b, :])
                dve.drain()
                for b in range(XG):
                    dve.bn_aggr(mv1[:, o + 2 * b:o + 2 * b + 2], bn1[:, b * 6:(b + 1) * 6])
                dve.drain()
                dve.tensor_scalar(mv1[:, o + 1:o + 2 * XG:2], mv1[:, o + 1:o + 2 * XG:2], EPS, None,
                                  ALU.add).then_inc(var1_ready, 1)

            stats(0)
            for g in range(NG):
                s = g % 2
                o = s * 2 * XG
                xn_g = xn[s][:, :].rearrange("p (b d) -> p b d", d=D)
                x_g = xin[g % 3][:, :].rearrange("p (b d) -> p b d", d=D)
                if g + 1 < NG:
                    stats(g + 1)
                dve.wait_ge(ln1_ready, g + 1)
                newton(rstd1[:, g * XG:(g + 1) * XG], mv1[:, o + 1:o + 2 * XG:2], nt1[:, o + XG:o + 2 * XG],
                       nt1[:, o:o + XG])
                dve.drain()
                if g >= 2:
                    dve.wait_ge(hi_copied, g - 1)
                    dve.wait_ge(low_done, g - 1)
                for b in range(XG):
                    c = g * XG + b
                    mm = dve.tensor_scalar(xn_g[:, b, :], x_g[:, b, :], mv1[:, o + 2 * b:o + 2 * b + 1], rstd1[:, c:c + 1],
                                           ALU.subtract, ALU.mult)
                mm.then_inc(xn_ready, 1)
                dve.scalar_tensor_tensor(out=off1[:, g * XG:(g + 1) * XG], in0=mv1[:, o:o + 2 * XG:2], scalar=-1.0,
                                         in1=rstd1[:, g * XG:(g + 1) * XG], op0=ALU.mult, op1=ALU.mult)
                dve.drain().then_inc(xin_used, 1)
                dve.tensor_tensor(r1[s][:, :], xn[s][:, :],
                                  xn[s][:, :].bitcast(BF16).rearrange("p (d t) -> p d t", t=2)[:, :, 1],
                                  ALU.subtract).then_inc(r1_ready, 1)
                if g == 1:
                    edge_lists()
                if g == 2:
                    slot_tables()
            dve.wait_ge(consts, 1)

            dve.wait_ge(edges_copied, 5)

            def quad_rows(q, k):
                dve.tensor_copy(idx[:, k * TQ:(k + 1) * TQ], src_t[:, ds(q, 1), :]).then_inc(idx_ready, 1)

            def select(q, s, b):
                dve.scalar_tensor_tensor(
                    out=sel[:, s, :, :], in0=lane[:, :].rearrange("p (j m) -> p j m", j=1).to_broadcast((P, TQ, P)),
                    scalar=block0[:, ds(b, 1)],
                    in1=dst_t[:, ds(q, 1), :].rearrange("p q j -> p (q j)").rearrange("p (j m) -> p j m", m=1)
                    .to_broadcast((P, TQ, P)),
                    op0=ALU.add, op1=ALU.is_equal).then_inc(sel_ready, 1)

            def add(s, b):
                to = acc[:, ds(b * AW, AW)]
                dve.tensor_tensor(to, to, ps_q[s][:, 0:AW], ALU.add).then_inc(acc_done, 1)

            n = dve.alloc_register("visits")
            b = dve.alloc_register("visit_block")
            pending = dve.alloc_register("pending_block")
            regs = [dve.alloc_register(f"quad_blocks{i}") for i in range(2 * QS)]
            dve.reg_mov(n, 0)
            dve.reg_mov(pending, 0)
            for q in range(3):
                quad_rows(q, q)
            dve.drain()
            blk = dve.alloc_register("node_block")
            last, end, t_reg = (dve.alloc_register(m) for m in ("last_node_slot", "chunk_end", "slot"))

            def select_quad(t, k):
                dve.reg_mov(b, regs[2 * k])
                with dve.While(lambda: dve.snap(b) < dve.snap(regs[2 * k + 1])):
                    to = dve.snap(b, min_val=0, max_val=NB - 1)
                    q = dve.snap(t * QS + k, min_val=0, max_val=NQ)
                    dve.drain()
                    dve.wait_ge(visit_done, dve.snap(n) + 2)
                    select(q, (k + 1) % 2, to)
                    add((k + 1) % 2, dve.snap(pending, min_val=0, max_val=NB - 1))
                    dve.reg_mov(pending, b)
                    dve.reg_add(n, n, 1)
                    dve.reg_add(b, b, 1)
                to = dve.snap(b, min_val=0, max_val=NB - 1)
                q = dve.snap(t * QS + k, min_val=0, max_val=NQ)
                dve.drain()
                dve.wait_ge(visit_done, dve.snap(n) + 1)
                select(q, k % 2, to)

            def add_last(t, k):
                dve.wait_ge(visit_done, dve.snap(n) + 2)
                add((k + 1) % 2, dve.snap(pending, min_val=0, max_val=NB - 1))
                dve.reg_mov(pending, b)
                dve.reg_add(n, n, 1)
                quad_rows(t * QS + k + 3, (k + 3) % QS)

            def block_of(t, known):
                if known is None:
                    dve.load([blk], ntab[0:1, ds(t, 1)])
                    return dve.snap(blk, min_val=0, max_val=NB - 2)
                return known

            def prepare_node(t, known=None):
                c = block_of(t, known)
                dve.tensor_copy(sm[:, 26:27], node_id[:, ds(c, 1)])
                dve.tensor_scalar(sm[:, 21:22], acc[:, ds(c * AW + D, 1)], 1.0, None, ALU.max)
                dve.drain()
                dve.reciprocal(sm[:, 21:22], sm[:, 21:22]).then_inc(deg_ready, 1)

            def chains(*steps):
                steps = [list(c) for c in steps if c]
                for r in range(max([len(c) for c in steps], default=0)):
                    if r:
                        dve.drain()
                    for c in steps:
                        if r < len(c):
                            c[r]()

            def nothing():
                pass

            def finish_row(t):
                def s0():
                    dve.wait_ge(count_ps, t + 1)
                    dve.tensor_tensor(g8[:, 6, :], ps_b[:, D:D + EX], seen[:, :], ALU.add)
                    dve.tensor_scalar(sm[:, 24:25], sm[:, 19:20], float(-SLOTS), float((EX + RV) * SLOTS - 1),
                                      ALU.mult, ALU.add)

                def s1():
                    dve.tensor_tensor(g8[:, 6, :], g8[:, 6, :], hot[:, :], ALU.mult)
                    dve.tensor_tensor(seen[:, :], ps_b[:, D + EX:D + 2 * EX], seen[:, :], ALU.add)

                def s2():
                    dve.tensor_reduce(sm[:, 22:23], g8[:, 6, :], AX, ALU.max)

                def s3():
                    dve.tensor_scalar(sm[:, 23:24], sm[:, 22:23], float(CAP), float(EX * SLOTS), ALU.is_gt, ALU.mult)
                    dve.tensor_tensor(sm[:, 24:25], sm[:, 22:23], sm[:, 24:25], ALU.add)

                def s4():
                    dve.tensor_tensor(slot[:, :], sm[:, 23:24], sm[:, 24:25], ALU.add).then_inc(row_ready, 1)

                return [s0, s1, s2, s3, s4]

            def new_row(t):
                dve.wait_ge(norm_ready, t + 1)
                half_newton(sm[:, 0:1], sm[:, 2:3], sm[:, 3:4])
                dve.drain()
                dve.tensor_tensor(sm[:, 4:5], sm[:, 3:4], sm[:, 2:3], ALU.mult)
                dve.drain()
                dve.wait_ge(x1_out, 16 * (t + 1))
                dve.wait_ge(disp_out, 16 * (t + 1))
                dve.scalar_tensor_tensor(out=row[:, 0:D], in0=ps_a[:, 0:KD, :].rearrange("p k d -> p (k d)"), scalar=sm[:, 4:5], in1=xb[:, :],
                                         op0=ALU.mult, op1=ALU.add)
                dve.tensor_copy(row[:, C_NODE:C_NODE + 1], sm[:, 26:27])
                dve.drain().then_inc(xb_free, 1)
                dve.tensor_tensor(row[:, 0:D], row[:, 0:D], gb_sb[:, :], ALU.add).then_inc(x1_ready, 1)
                dve.drain()
                dve.bn_stats(bn[:, :], row[:, 0:D])
                dve.drain()
                dve.bn_aggr(sm[:, 8:10], bn[:, :])
                dve.drain()
                dve.tensor_scalar(sm[:, 10:11], sm[:, 9:10], EPS, None, ALU.add).then_inc(var2_ready, 1)

            def normalise_row(t):
                dve.wait_ge(ln2_ready, t + 1)
                half_newton(sm[:, 10:11], sm[:, 12:13], sm[:, 13:14])
                dve.tensor_scalar(sm[:, 14:15], sm[:, 8:9], sm[:, 12:13], -1.0, ALU.mult, ALU.mult)
                dve.drain()
                dve.tensor_tensor(row[:, C_RSTD:C_RSTD + 1], sm[:, 13:14], sm[:, 12:13], ALU.mult)
                dve.tensor_tensor(row[:, C_OFF:C_OFF + 1], sm[:, 13:14], sm[:, 14:15], ALU.mult)
                dve.drain().then_inc(stat2_ready, 1)

            def route(t):
                def s0():
                    dve.wait_ge(logit_ps, t + 1)
                    dve.tensor_tensor(g8[:, 0, :], ps_b[:, D + 2 * EX:D + 3 * EX], gateb_sb[:, :], ALU.add)

                def s1():
                    dve.tensor_reduce(sm[:, 16:17], g8[:, 0, :], AX, ALU.max, negate=True).then_inc(logit_ready, 1)

                def s2():
                    dve.wait_ge(exp_ready, t + 1)
                    dve.reciprocal(sm[:, 18:19], sm[:, 17:18])

                def s3():
                    dve.tensor_scalar(g8[:, 2, :], g8[:, 1, :], sm[:, 18:19], None, ALU.mult)

                def s4():
                    dve.tensor_reduce(row[:, C_GATE:C_GATE + 1], g8[:, 2, :], AX, ALU.max)

                def s5():
                    dve.scalar_tensor_tensor(out=g8[:, 3, :], in0=g8[:, 2, :], scalar=row[:, C_GATE:C_GATE + 1],
                                             in1=rev9[:, :], op0=ALU.is_equal, op1=ALU.mult)

                def s6():
                    dve.tensor_reduce(sm[:, 25:26], g8[:, 3, :], AX, ALU.max)

                def s7():
                    dve.tensor_scalar(sm[:, 19:20], sm[:, 25:26], valid[:, ds(t, 1)], None, ALU.mult)

                def s8():
                    dve.tensor_scalar(hot[:, :], rev9[:, :], sm[:, 19:20], None, ALU.is_equal).then_inc(hot_ready, 1)

                return [s0, s1, s2, s3, s4, s5, s6, s7, s8]

            def choose(t, whole=True):
                lim, least = (float((CAP // P) * P), float(P)) if whole else (float(CAP), 1.0)
                have, cand, hit, take = (g8[0:1, r, :] for r in (4, 5, 4, 7))

                def s0():
                    dve.scalar_tensor_tensor(out=have, in0=seen[0:1, :], scalar=lim, in1=taken[:, :],
                                             op0=ALU.min, op1=ALU.subtract)

                def s1():
                    dve.scalar_tensor_tensor(out=cand, in0=have, scalar=least, in1=rev[0:1, :],
                                             op0=ALU.is_ge, op1=ALU.mult)

                def s2():
                    dve.tensor_reduce(sm[0:1, 27:28], cand, AX, ALU.max)

                def s3():
                    dve.tensor_scalar(hit, rev[0:1, :], sm[0:1, 27:28], None, ALU.is_equal)
                    dve.tensor_scalar(sm[0:1, 28:29], sm[0:1, 27:28], 1.0, -1.0, ALU.max, ALU.mult)

                def s4():
                    dve.tensor_tensor(take, hit, taken[:, :], ALU.mult)
                    dve.tensor_scalar(ctab[0:1, ds(t + 1, 1), 1], sm[0:1, 28:29], float(EX), None, ALU.add)

                def s5():
                    dve.tensor_reduce(sm[0:1, 29:30], take, AX, ALU.max)
                    dve.scalar_tensor_tensor(out=taken[:, :], in0=hit, scalar=float(P), in1=taken[:, :],
                                             op0=ALU.mult, op1=ALU.add)

                def s6():
                    dve.scalar_tensor_tensor(out=sm[0:1, 30:31], in0=sm[0:1, 27:28], scalar=float(-SLOTS),
                                             in1=sm[0:1, 29:30], op0=ALU.mult, op1=ALU.add)

                def s7():
                    dve.tensor_scalar(ctab[0:1, ds(t + 1, 1), 0], sm[0:1, 30:31], float(EX * SLOTS), None, ALU.add)

                def s8():
                    dve.sem_inc(code_ready, 1)

                return [s0, s1, s2, s3, s4, s5, s6, s7, s8]

            def result(t, node):
                c = chunks(t)
                y, keep, lim = b2_b, cat[:, 0:D], cat[:, D:2 * D]

                def s0():
                    if node:
                        dve.wait_ge(cat_ps, t + 1)
                    dve.wait_ge(y_ready, c)
                    dve.wait_ge(ys_in, 32 * c)
                    dve.tensor_tensor(y[:, :], ps_b[:, 0:D], b2_b[:, :], ALU.add).then_inc(y_read, 1)

                def s1():
                    dve.tensor_scalar(y[:, :], y[:, :], ys[:, C_GATE:C_GATE + 1], None, ALU.mult)

                def s2():
                    dve.tensor_scalar(lim, y[:, :], -1e4, 1e4, ALU.max, ALU.min)
                    dve.tensor_tensor(keep, y[:, :], y[:, :], ALU.is_equal)

                def s3():
                    dve.tensor_tensor(lim, lim, keep, ALU.mult)

                def s4():
                    dve.tensor_scalar(keep.bitcast(I32), y[:, :], 0.0, 0.0, ALU.mult, ALU.is_equal)

                def s5():
                    dve.copy_predicated(lim, keep.bitcast(I32), y[:, :])
                    dve.tensor_copy(node_i[:, :], ys[:, C_NODE:C_NODE + 1])

                def s6():
                    dve.tensor_tensor(ys[:, 0:D], lim, ys[:, 0:D], ALU.add)

                def s7():
                    dve.sem_inc(res_ready, 1)

                return [s0, s1, s2, s3, s4, s5, s6, s7]

            def trip(t, quads=True, node=True, prev=True, chunk=True, next_node=True, next_known=None):
                if quads:
                    dve.wait_ge(cat_ready, t + 1)
                    add_last(t, 0)
                    select_quad(t, 1)
                chains(route(t) if prev else [], choose(t, whole=prev) if chunk else [])
                if quads:
                    add_last(t, 1)
                    select_quad(t, 2)
                chains(result(t, node) if chunk else [],
                       ([nothing] * 3 if chunk else []) + finish_row(t) if prev else [])
                if quads:
                    add_last(t, 2)
                    select_quad(t, 3)
                    dve.load(regs, qtab[0:1, ds(t * QS + QS, QS), :])
                if node:
                    new_row(t)
                if quads:
                    add_last(t, 3)
                if node:
                    normalise_row(t)
                if quads:
                    select_quad(t + 1, 0)
                if node and next_node:
                    prepare_node(t + 1, next_known)

            dve.wait_ge(const_in, 16 * 4)
            prepare_node(0)
            dve.load(regs, qtab[0:1, 0:QS, :])
            select_quad(dve.snap(n), 0)
            with dve.Fori(0, C0) as t:
                trip(t, chunk=False)
            with dve.Fori(C0, TRIPS) as t:
                trip(t)
            dve.drain()
            dve.wait_ge(visit_done, dve.snap(n) + 2)
            add((NQ - 1) % 2, dve.snap(pending, min_val=0, max_val=NB - 1))
            dve.drain()
            dve.load([last], ends[0:1, 0:1])
            dve.reg_mov(t_reg, TRIPS)
            with dve.While(lambda: dve.snap(t_reg) + 1 < dve.snap(last)):
                trip(dve.snap(t_reg, min_val=TRIPS, max_val=TABW - 4), quads=False)
                dve.reg_add(t_reg, t_reg, 1)
            trip(dve.snap(t_reg, min_val=TRIPS, max_val=TABW - 4), quads=False, next_known=NB - 1)
            dve.reg_add(t_reg, t_reg, 1)
            trip(dve.snap(t_reg, min_val=TRIPS, max_val=TABW - 3), quads=False, next_node=False)
            dve.reg_add(t_reg, t_reg, 1)
            trip(dve.snap(t_reg, min_val=TRIPS, max_val=TABW - 2), quads=False, node=False)
            dve.reg_add(t_reg, t_reg, 1)
            dve.drain()
            dve.tensor_scalar(g8[0:1, 4, :], seen[0:1, :], float(CAP), float(P - 1), ALU.min, ALU.add)
            dve.drain()
            dve.tensor_copy(left_i[:, :], g8[0:1, 4, :])
            dve.drain()
            dve.tensor_scalar(left_i[:, :], left_i[:, :], 7, None, ALU.logical_shift_right)
            dve.drain()
            dve.tensor_copy(g8[0:1, 5, :], left_i[:, :])
            dve.drain()
            dve.scalar_tensor_tensor(out=g8[0:1, 7, :], in0=taken[:, :], scalar=-1.0 / P, in1=g8[0:1, 5, :],
                                     op0=ALU.mult, op1=ALU.add)
            dve.drain()
            dve.tensor_reduce(sm[0:1, 27:28], g8[0:1, 7, :], AX, ALU.add)
            dve.drain()
            dve.scalar_tensor_tensor(out=sm[0:1, 28:29], in0=sm[0:1, 27:28], scalar=3.0, in1=last_f[:, :],
                                     op0=ALU.add, op1=ALU.add)
            dve.drain()
            dve.tensor_copy(ends[0:1, 1:2], sm[0:1, 28:29])
            dve.drain().then_inc(ends_ready, 1)
            dve.load([end], ends[0:1, 1:2])
            with dve.While(lambda: dve.snap(t_reg) < dve.snap(end)):
                trip(dve.snap(t_reg, min_val=TRIPS, max_val=NSLOTS - 4), quads=False, node=False, prev=False)
                dve.reg_add(t_reg, t_reg, 1)
            chains(result(dve.snap(t_reg), False))


_INS = ["x", "src", "dst", "L0_gnn_weight", "L0_gnn_bias", "L0_ffn_gate_w", "L0_ffn_gate_b",
        "L0_ffn_w1", "L0_ffn_b1", "L0_ffn_w2", "L0_ffn_b2"]


def kernel(**inputs):
    import concourse.bacc as _bacc
    from concourse.bass_utils import run_bass_kernel_spmd as _run

    nc = _bacc.Bacc("TRN2", target_bir_lowering=False, num_devices=1, dynamic_dma_scratch_size=2048)
    arrays, args = {}, []
    for name in _INS:
        a = np.ascontiguousarray(inputs[name])
        arrays[f"in_{name}"] = a
        args.append(nc.dram_tensor(f"in_{name}", a.shape, mybir.dt.from_np(a.dtype), kind="ExternalInput").ap())
    args.append(nc.dram_tensor("out_0", (N, D), FP32, kind="ExternalOutput").ap())
    gnn_moe_layer(nc, *args)
    r = _run(nc, [arrays], core_ids=[0])
    return r.results[0]["out_0"]
```
